# Optimizing a Trainium2 kernel written in Bass

```python
import numpy as np
import jax
import jax.numpy as jnp

def _softmax(x, axis=-1):
    return jax.nn.softmax(x, axis=axis)

def _gelu(x):
    return jax.nn.gelu(x, approximate=True)

def _silu(x):
    return jax.nn.silu(x)

def _sigmoid(x):
    return jax.nn.sigmoid(x)

def _layernorm(x, axis=-1, eps=1e-05):
    m = jnp.mean(x, axis=axis, keepdims=True)
    v = jnp.var(x, axis=axis, keepdims=True)
    return (x - m) / jnp.sqrt(v + eps)

def _scatter_add(tgt, idx, src, axis=0):
    return tgt.at[idx].add(src)

def _segment_sum(src, seg, n):
    return jax.ops.segment_sum(src, seg, n)
kernel_name = 'mk_pixart_seq_d2_seqx_r4_59a305'

def setup_inputs(seed: int=0):
    np.random.seed(seed)
    _w = jnp.asarray

    def _rec_inputs():
        import jax
        import jax.numpy as jnp
        _rk = jax.random.key(seed)
        x = -0.0003929 + 0.9999 * jax.random.normal(jax.random.fold_in(_rk, 1), (16, 256, 256), jnp.float32)
        _lenS = 256 - jax.random.randint(jax.random.fold_in(_rk, 7), (16,), 0, max(1, 256 // 4) + 1, jnp.int32)
        _lenS2 = 256 - jax.random.randint(jax.random.fold_in(_rk, 8), (16,), 0, max(1, 256 // 4) + 1, jnp.int32)
        _ctx_1024P = jax.random.normal(jax.random.fold_in(_rk, 11), (16, 16, 256), jnp.float32)
        _ctx_1024c = jax.random.dirichlet(jax.random.fold_in(_rk, 511), 0.3 * jnp.ones((16,), jnp.float32), (16, 256))
        _ctx_1024t = jnp.einsum('bsk,bkd->bsd', _ctx_1024c, _ctx_1024P)
        _ctx_1024t = _ctx_1024t * jax.lax.rsqrt(jnp.mean(jnp.square(_ctx_1024t)) + 1e-12) * 0.953939
        ctx_1024 = -1.39393e-06 + 0.999914 * (_ctx_1024t + 0.3 * jax.random.normal(jax.random.fold_in(_rk, 611), (16, 256, 256), jnp.float32))
        cond_1024 = -0.00920427 + 1.00102 * jax.random.normal(jax.random.fold_in(_rk, 12), (16, 256), jnp.float32)
        return (x, ctx_1024, cond_1024)
    x, ctx_1024, cond_1024 = _rec_inputs()

    def _L0_xcond_setup():
        import jax, jax.numpy as jnp
        import numpy as np
        EPS = 1e-05

        def _ada_ln(x, c, W_ss, b_ss):
            mu = jnp.mean(x, axis=-1, keepdims=True)
            var = jnp.mean((x - mu) ** 2, axis=-1, keepdims=True)
            h = (x - mu) / jnp.sqrt(var + EPS)
            ss = jax.nn.silu(c) @ W_ss + b_ss
            scale, bias = jnp.split(ss, 2, axis=-1)
            return (1.0 + scale)[:, None, :] * h + bias[:, None, :]
        key = jax.random.key(seed)
        ks = jax.random.split(key, 12)
        B, Lq, Lkv, H = (8, 512, 128, 256)
        s = 0.02
        return {'x_q': jax.random.normal(ks[0], (B, Lq, H), jnp.float32), 'x_kv': jax.random.normal(ks[1], (B, Lkv, H), jnp.float32), 't_vec': jax.random.normal(ks[2], (B, H), jnp.float32), 'Wq': jax.random.normal(ks[3], (H, H), jnp.float32) * s, 'bq': jnp.zeros((H,), jnp.float32), 'Wkv': jax.random.normal(ks[4], (H, 2 * H), jnp.float32) * s, 'bkv': jnp.zeros((2 * H,), jnp.float32), 'Wp': jax.random.normal(ks[5], (H, H), jnp.float32) * s, 'bp': jnp.zeros((H,), jnp.float32), 'Wss_q': jax.random.normal(ks[6], (H, 2 * H), jnp.float32) * s, 'bss_q': jnp.zeros((2 * H,), jnp.float32), 'Wss_kv': jax.random.normal(ks[7], (H, 2 * H), jnp.float32) * s, 'bss_kv': jnp.zeros((2 * H,), jnp.float32)}
    _L0_xcond_all = _L0_xcond_setup()
    _L0_xcond_in = {k: v for k, v in _L0_xcond_all.items() if k in ('Wq', 'bq', 'Wkv', 'bkv', 'Wp', 'bp', 'Wss_q', 'bss_q', 'Wss_kv', 'bss_kv')}
    del _L0_xcond_all

    def _L1_xcond_setup():
        import jax, jax.numpy as jnp
        import numpy as np
        C = 256
        H = 16
        D = C // H
        WIN = 128
        SHIFT = 64
        TOPK = 16
        HID = 1024
        EPS = 1e-06

        def _ln(x):
            x32 = x.astype(jnp.float32)
            m = x32.mean(-1, keepdims=True)
            v = jnp.mean((x32 - m) ** 2, axis=-1, keepdims=True)
            return ((x32 - m) * jax.lax.rsqrt(v + EPS)).astype(x.dtype)

        def _self_attn(h, w_qkv, b_qkv, w_so, b_so):
            B, L, _ = h.shape
            qkv = h @ w_qkv + b_qkv
            qkv = jnp.roll(qkv, -SHIFT, axis=1)
            nw = L // WIN
            qkv = qkv.reshape(B, nw, WIN, 3, H, D)
            q, k, v = (qkv[:, :, :, 0], qkv[:, :, :, 1], qkv[:, :, :, 2])
            scores = jnp.einsum('bnqhd,bnkhd->bnhqk', q, k) / jnp.sqrt(jnp.float32(D)).astype(h.dtype)
            attn = jax.nn.softmax(scores, axis=-1)
            o = jnp.einsum('bnhqk,bnkhd->bnqhd', attn, v).reshape(B, L, C)
            o = jnp.roll(o, SHIFT, axis=1)
            return o @ w_so + b_so

        def _topk_cross_attn(h, ctx, w_q, b_q, w_kv, b_kv, w_co, b_co):
            B, L, _ = h.shape
            Lc = ctx.shape[1]
            q = (h @ w_q + b_q).reshape(B, L, H, D)
            kv = (ctx @ w_kv + b_kv).reshape(B, Lc, 2, H, D)
            k, v = (kv[:, :, 0], kv[:, :, 1])
            scores = jnp.einsum('bqhd,bkhd->bhqk', q, k) / jnp.sqrt(jnp.float32(D)).astype(h.dtype)
            top_s, top_i = jax.lax.top_k(scores, TOPK)
            attn = jax.nn.softmax(top_s, axis=-1)
            v_bh = jnp.transpose(v, (0, 2, 1, 3))
            vg = jnp.take_along_axis(v_bh[:, :, None, :, :], top_i[..., None], axis=3)
            o = jnp.einsum('bhqk,bhqkd->bqhd', attn, vg).reshape(B, L, C)
            return o @ w_co + b_co

        def _swiglu(h, w_m1, b_m1, w_m2, b_m2):
            u = h @ w_m1 + b_m1
            a, b = (u[..., :HID], u[..., HID:])
            return jax.nn.silu(a) * b @ w_m2 + b_m2
        key = jax.random.key(seed)
        ks = jax.random.split(key, 24)
        s = 0.02
        inp = {'x': jax.random.normal(ks[0], (2, 1024, C), jnp.float32), 'mod': jax.random.normal(ks[1], (2, C), jnp.float32), 'context': jax.random.normal(ks[2], (2, 256, C), jnp.float32), 'w_ada': jax.random.normal(ks[3], (C, 9 * C), jnp.float32) * s, 'b_ada': jnp.zeros((9 * C,), jnp.float32), 'w_qkv': jax.random.normal(ks[4], (C, 3 * C), jnp.float32) * s, 'b_qkv': jnp.zeros((3 * C,), jnp.float32), 'w_so': jax.random.normal(ks[5], (C, C), jnp.float32) * s, 'b_so': jnp.zeros((C,), jnp.float32), 'w_q': jax.random.normal(ks[6], (C, C), jnp.float32) * s, 'b_q': jnp.zeros((C,), jnp.float32), 'w_kv': jax.random.normal(ks[7], (C, 2 * C), jnp.float32) * s, 'b_kv': jnp.zeros((2 * C,), jnp.float32), 'w_co': jax.random.normal(ks[8], (C, C), jnp.float32) * s, 'b_co': jnp.zeros((C,), jnp.float32), 'w_m1': jax.random.normal(ks[9], (C, 2 * HID), jnp.float32) * s, 'b_m1': jnp.zeros((2 * HID,), jnp.float32), 'w_m2': jax.random.normal(ks[10], (HID, C), jnp.float32) * s, 'b_m2': jnp.zeros((C,), jnp.float32)}
        return inp
    _L1_xcond_all = _L1_xcond_setup()
    _L1_xcond_in = {k: v for k, v in _L1_xcond_all.items() if k in ('w_ada', 'b_ada', 'w_qkv', 'b_qkv', 'w_so', 'b_so', 'w_q', 'b_q', 'w_kv', 'b_kv', 'w_co', 'b_co', 'w_m1', 'b_m1', 'w_m2', 'b_m2')}
    del _L1_xcond_all
    return {'x': x, 'ctx_1024': ctx_1024, 'cond_1024': cond_1024, 'L0_xcond_Wq': _L0_xcond_in['Wq'], 'L0_xcond_bq': _L0_xcond_in['bq'], 'L0_xcond_Wkv': _L0_xcond_in['Wkv'], 'L0_xcond_bkv': _L0_xcond_in['bkv'], 'L0_xcond_Wp': _L0_xcond_in['Wp'], 'L0_xcond_bp': _L0_xcond_in['bp'], 'L0_xcond_Wss_q': _L0_xcond_in['Wss_q'], 'L0_xcond_bss_q': _L0_xcond_in['bss_q'], 'L0_xcond_Wss_kv': _L0_xcond_in['Wss_kv'], 'L0_xcond_bss_kv': _L0_xcond_in['bss_kv'], 'L1_xcond_w_ada': _L1_xcond_in['w_ada'], 'L1_xcond_b_ada': _L1_xcond_in['b_ada'], 'L1_xcond_w_qkv': _L1_xcond_in['w_qkv'], 'L1_xcond_b_qkv': _L1_xcond_in['b_qkv'], 'L1_xcond_w_so': _L1_xcond_in['w_so'], 'L1_xcond_b_so': _L1_xcond_in['b_so'], 'L1_xcond_w_q': _L1_xcond_in['w_q'], 'L1_xcond_b_q': _L1_xcond_in['b_q'], 'L1_xcond_w_kv': _L1_xcond_in['w_kv'], 'L1_xcond_b_kv': _L1_xcond_in['b_kv'], 'L1_xcond_w_co': _L1_xcond_in['w_co'], 'L1_xcond_b_co': _L1_xcond_in['b_co'], 'L1_xcond_w_m1': _L1_xcond_in['w_m1'], 'L1_xcond_b_m1': _L1_xcond_in['b_m1'], 'L1_xcond_w_m2': _L1_xcond_in['w_m2'], 'L1_xcond_b_m2': _L1_xcond_in['b_m2']}

def reference(x, ctx_1024, cond_1024, L0_xcond_Wq, L0_xcond_bq, L0_xcond_Wkv, L0_xcond_bkv, L0_xcond_Wp, L0_xcond_bp, L0_xcond_Wss_q, L0_xcond_bss_q, L0_xcond_Wss_kv, L0_xcond_bss_kv, L1_xcond_w_ada, L1_xcond_b_ada, L1_xcond_w_qkv, L1_xcond_b_qkv, L1_xcond_w_so, L1_xcond_b_so, L1_xcond_w_q, L1_xcond_b_q, L1_xcond_w_kv, L1_xcond_b_kv, L1_xcond_w_co, L1_xcond_b_co, L1_xcond_w_m1, L1_xcond_b_m1, L1_xcond_w_m2, L1_xcond_b_m2):
    import jax
    import jax.numpy as jnp

    def _L0_xcond_ref(x_q, x_kv, t_vec, Wq, bq, Wkv, bkv, Wp, bp, Wss_q, bss_q, Wss_kv, bss_kv):
        import jax, jax.numpy as jnp
        import numpy as np
        EPS = 1e-05

        def _ada_ln(x, c, W_ss, b_ss):
            mu = jnp.mean(x, axis=-1, keepdims=True)
            var = jnp.mean((x - mu) ** 2, axis=-1, keepdims=True)
            h = (x - mu) / jnp.sqrt(var + EPS)
            ss = jax.nn.silu(c) @ W_ss + b_ss
            scale, bias = jnp.split(ss, 2, axis=-1)
            return (1.0 + scale)[:, None, :] * h + bias[:, None, :]
        B, Lq, H = x_q.shape
        Lkv = x_kv.shape[1]
        nh = 16
        dh = H // nh
        xq = _ada_ln(x_q, t_vec, Wss_q, bss_q)
        xkv = _ada_ln(x_kv, t_vec, Wss_kv, bss_kv)
        q = (xq @ Wq + bq).reshape(B, Lq, nh, dh)
        kv = (xkv @ Wkv + bkv).reshape(B, Lkv, 2, nh, dh)
        k = kv[:, :, 0]
        v = kv[:, :, 1]
        scores = jnp.einsum('bqhd,bkhd->bhqk', q, k) / jnp.sqrt(jnp.float32(dh))
        attn = jax.nn.softmax(scores, axis=-1)
        out = jnp.einsum('bhqk,bkhd->bqhd', attn, v).reshape(B, Lq, H)
        return x_q + (out @ Wp + bp)

    def _L1_xcond_ref(x, mod, context, w_ada, b_ada, w_qkv, b_qkv, w_so, b_so, w_q, b_q, w_kv, b_kv, w_co, b_co, w_m1, b_m1, w_m2, b_m2):
        import jax, jax.numpy as jnp
        import numpy as np
        C = 256
        H = 16
        D = C // H
        WIN = 128
        SHIFT = 64
        TOPK = 16
        HID = 1024
        EPS = 1e-06

        def _ln(x):
            x32 = x.astype(jnp.float32)
            m = x32.mean(-1, keepdims=True)
            v = jnp.mean((x32 - m) ** 2, axis=-1, keepdims=True)
            return ((x32 - m) * jax.lax.rsqrt(v + EPS)).astype(x.dtype)

        def _self_attn(h, w_qkv, b_qkv, w_so, b_so):
            B, L, _ = h.shape
            qkv = h @ w_qkv + b_qkv
            qkv = jnp.roll(qkv, -SHIFT, axis=1)
            nw = L // WIN
            qkv = qkv.reshape(B, nw, WIN, 3, H, D)
            q, k, v = (qkv[:, :, :, 0], qkv[:, :, :, 1], qkv[:, :, :, 2])
            scores = jnp.einsum('bnqhd,bnkhd->bnhqk', q, k) / jnp.sqrt(jnp.float32(D)).astype(h.dtype)
            attn = jax.nn.softmax(scores, axis=-1)
            o = jnp.einsum('bnhqk,bnkhd->bnqhd', attn, v).reshape(B, L, C)
            o = jnp.roll(o, SHIFT, axis=1)
            return o @ w_so + b_so

        def _topk_cross_attn(h, ctx, w_q, b_q, w_kv, b_kv, w_co, b_co):
            B, L, _ = h.shape
            Lc = ctx.shape[1]
            q = (h @ w_q + b_q).reshape(B, L, H, D)
            kv = (ctx @ w_kv + b_kv).reshape(B, Lc, 2, H, D)
            k, v = (kv[:, :, 0], kv[:, :, 1])
            scores = jnp.einsum('bqhd,bkhd->bhqk', q, k) / jnp.sqrt(jnp.float32(D)).astype(h.dtype)
            top_s, top_i = jax.lax.top_k(scores, TOPK)
            attn = jax.nn.softmax(top_s, axis=-1)
            v_bh = jnp.transpose(v, (0, 2, 1, 3))
            vg = jnp.take_along_axis(v_bh[:, :, None, :, :], top_i[..., None], axis=3)
            o = jnp.einsum('bhqk,bhqkd->bqhd', attn, vg).reshape(B, L, C)
            return o @ w_co + b_co

        def _swiglu(h, w_m1, b_m1, w_m2, b_m2):
            u = h @ w_m1 + b_m1
            a, b = (u[..., :HID], u[..., HID:])
            return jax.nn.silu(a) * b @ w_m2 + b_m2
        m = jax.nn.silu(mod) @ w_ada + b_ada
        sh_msa, sc_msa, g_msa, sh_mca, sc_mca, g_mca, sh_mlp, sc_mlp, g_mlp = [m[:, i * C:(i + 1) * C][:, None, :] for i in range(9)]
        h = _ln(x) * (1 + sc_msa) + sh_msa
        h = _self_attn(h, w_qkv, b_qkv, w_so, b_so)
        x = x + h * g_msa
        h = _ln(x) * (1 + sc_mca) + sh_mca
        h = _topk_cross_attn(h, context, w_q, b_q, w_kv, b_kv, w_co, b_co)
        x = x + h * g_mca
        h = _ln(x) * (1 + sc_mlp) + sh_mlp
        h = _swiglu(h, w_m1, b_m1, w_m2, b_m2)
        x = x + h * g_mlp
        return x
    x = _L0_xcond_ref(x, ctx_1024, cond_1024, L0_xcond_Wq, L0_xcond_bq, L0_xcond_Wkv, L0_xcond_bkv, L0_xcond_Wp, L0_xcond_bp, L0_xcond_Wss_q, L0_xcond_bss_q, L0_xcond_Wss_kv, L0_xcond_bss_kv)
    x = _L1_xcond_ref(x, cond_1024, ctx_1024, L1_xcond_w_ada, L1_xcond_b_ada, L1_xcond_w_qkv, L1_xcond_b_qkv, L1_xcond_w_so, L1_xcond_b_so, L1_xcond_w_q, L1_xcond_b_q, L1_xcond_w_kv, L1_xcond_b_kv, L1_xcond_w_co, L1_xcond_b_co, L1_xcond_w_m1, L1_xcond_b_m1, L1_xcond_w_m2, L1_xcond_b_m2)
    return x

_drawn_inputs = setup_inputs


def setup_inputs(seed=0):
    import zlib

    import numpy as np

    out = dict(_drawn_inputs(seed))
    spreads = {'L0_xcond_bq': (0.0, 2.0),
     'L0_xcond_bkv': (0.0, 0.1),
     'L0_xcond_bp': (0.0, 0.1),
     'L0_xcond_bss_q': (0.0, 0.8),
     'L0_xcond_bss_kv': (0.0, 0.662),
     'L1_xcond_b_ada': (0.0, 0.434),
     'L1_xcond_b_qkv': (0.0, 0.8),
     'L1_xcond_b_so': (0.0, 0.396),
     'L1_xcond_b_q': (0.0, 0.8),
     'L1_xcond_b_kv': (0.0, 0.8),
     'L1_xcond_b_co': (0.0, 0.399),
     'L1_xcond_b_m1': (0.0, 0.8),
     'L1_xcond_b_m2': (0.0, 1.676)}
    factors = {'L0_xcond_Wq': 8.0,
     'L0_xcond_Wss_q': 8.0,
     'L1_xcond_w_qkv': 8.0,
     'L1_xcond_w_so': 6.279,
     'L1_xcond_w_q': 5.289,
     'L1_xcond_w_kv': 3.675,
     'L1_xcond_w_co': 3.365,
     'L1_xcond_w_m1': 6.369,
     'L1_xcond_w_m2': 6.343}
    for name, (base, spread) in spreads.items():
        noise = np.random.default_rng([zlib.crc32(name.encode()), seed]).standard_normal(out[name].shape)
        drawn = base * np.exp(spread * noise) if base else spread * noise
        out[name] = jnp.asarray(drawn.astype(out[name].dtype))
    for name, factor in factors.items():
        out[name] = (out[name] * factor).astype(out[name].dtype)
    return out
```

```python
from contextlib import ExitStack

import concourse.bass as bass
from concourse import mybir

F32 = mybir.dt.float32
BF16 = mybir.dt.bfloat16
ALU = mybir.AluOpType
ACT = mybir.ActivationFunctionType
AX_X = mybir.AxisListType.X

P = 128
BIG = 1e30
CROSS, SELF, TOPK = 0, 1, 2
Q_PARTS = (0, 0, 0, 1, 1, 2)
K_PARTS = (0, 1, 2, 0, 1, 0)


class Signal:

    def __init__(self, sem, per, seed=0, unit=1):
        self.sem, self.per, self.seed, self.unit = sem, per, seed, unit

    def at(self, b, k):
        return b * (self.per * self.unit) + (self.seed + k) * self.unit

    def before(self, b, k):
        assert self.seed >= self.per
        return b * (self.per * self.unit) + (self.seed + k - self.per) * self.unit

    def room(self, b, n):
        assert self.unit == 1
        return b * self.per + n + 1


def build(nc, x, ctx_in, cond, Wq, bq, Wkv, bkv, Wp, bp, Wss_q, bss_q, Wss_kv, bss_kv, w_ada, b_ada,
          w_qkv, b_qkv, w_so, b_so, w_q, b_q, w_kv, b_kv, w_co, b_co, w_m1, b_m1, w_m2, b_m2, out):
    B, L, C = x.shape
    H, D = 16, 16
    NT = L // P
    NC = C // P
    HID = w_m2.shape[0]
    NJ = HID // P
    WIN, SHIFT = 128, 64
    HH = H // NC
    SCALE = float(D) ** -0.5
    NPART = 3
    KP = len(Q_PARTS) * D
    KM = KP + 2
    NS = H
    NW = L // WIN

    MODS = [(0, 0, 1), (0, C, 0), (1, 0, 1), (1, C, 0)] + [
        (2, i * C, one) for i, one in ((1, 1), (0, 0), (4, 1), (3, 0), (7, 1), (6, 0))]
    M_XQ, M_XKV, M_MSA, M_MCA, M_MLP = 0, 2, 4, 6, 8
    BIAS = [(bss_q, 0, 2 * C), (bss_kv, 0, 2 * C), (b_ada, 0, 9 * C), (bq, 0, C), (bkv, 0, C),
            (b_qkv, 0, 2 * C), (b_q, 0, C), (b_kv, 0, C), (b_m1, 0, 2 * HID)]
    row, BROW = 0, []
    for _, _, n in BIAS:
        BROW.append(row)
        row += n // P
    NROW = row
    R_SSQ, R_SSKV, R_ADA, R_Q0, R_K0, R_QK1, R_Q2, R_K2, R_M1 = BROW

    PJ = (["tx", "tc", "tr", "q0", "k0", "v0", "k2", "v2", "mt0", "o0",
           "th1", "q1", "k1", "v1", "mt1", "o1", "th2", "q2", "mt2", "o2", "th3"]
          + [f"h{j}" for j in range(NJ)] + ["o3"])
    assert len(PJ) % 2 == 0
    TENSORS = [t for t in PJ if t in ("q0", "k0", "k2", "q1", "k1", "q2")]

    SETUP_POOL = 11
    SETUP_DVE_GATES = 8 + len(MODS) * NC + 6
    SETUP_DVE = SETUP_DVE_GATES + 1
    ACT_STEPS = 12 + 2 + 12 + 3 + NJ
    DVE_STEPS = 10 + 3 * NT + 3 + 8 * NS + 14 + 1 + NJ + 3 * NT

    with ExitStack() as ctx:
        def sb(name, shape, dt=F32):
            return ctx.enter_context(nc.sbuf_tensor(name, shape, dt))

        def sem(name):
            return ctx.enter_context(nc.semaphore(name))

        def signal(name, per, seed=0, unit=1):
            s = Signal(sem(name), per, seed, unit)
            if seed:
                seeds.append(s)
            return s

        seeds = []
        parts_dram = {t: nc.dram_tensor(f"parts_{t}", (NPART, C, L), BF16, kind="Internal").ap() for t in TENSORS}
        gates_dram = nc.dram_tensor("gates_scratch", (B, 6 * C), F32, kind="Internal").ap()

        def weight(name, w):
            k, n = w.shape
            return sb(name, [P, k // P, n]), w.rearrange("(c p) n -> p c n", p=P)

        W = {}
        loads = []
        full = sb("full", [P, 2, NC, L])
        rest = sb("rest", [P, 2, NC, L])
        ada_other = sb("ada_other", [P, NC, 9 * C])
        W["wss0"] = full[:].rearrange("p s c l -> p (s c l)").rearrange("p (c n) -> p c n", c=NC)
        W["wss1"] = rest[:].rearrange("p s c l -> p (s c l)").rearrange("p (c n) -> p c n", c=NC)
        W["ada"] = ada_other[:]
        other = (ada_other[:].rearrange("p c n -> p (c n)")[:, 0:NT * H * L // 2].bitcast(BF16)
                 .rearrange("p (t h n) -> p t h n", t=NT, h=H))
        for name, w in (("wss0", Wss_q), ("wss1", Wss_kv), ("ada", w_ada)):
            loads.append((W[name], w.rearrange("(c p) n -> p c n", p=P)))
        for name, w in (("q0", Wq), ("kv0", Wkv), ("p0", Wp),
                        ("qkv1", w_qkv), ("p1", w_so), ("q2", w_q), ("kv2", w_kv), ("p2", w_co),
                        ("m1", w_m1), ("m2", w_m2)):
            W[name], src = weight("w_" + name, w)
            loads.append((W[name][:], src))
        bias_rows = sb("bias_rows", [NROW, P])
        for (v, o, n), r in zip(BIAS, BROW):
            loads.append((bias_rows[r:r + n // P, :], v[o:o + n].rearrange("(r p) -> r p", p=P)))
        vb = sb("vb", [P, 4, C])
        for i, v in enumerate((bkv[C:2 * C], b_qkv[2 * C:3 * C], b_kv[C:2 * C], bp)):
            loads.append((vb[:, i, :], v.partition_broadcast(P)))
        hid = sb("hid", [P, NJ, L])
        prob = sb("prob", [P, 4, 512])
        gate_bias = hid[0:B, 0:6, :]
        for i, v in enumerate([b_ada[g * C:(g + 1) * C] for g in (2, 5, 8)] + [b_so, b_co, b_m2]):
            loads.append((gate_bias[:, i, :], v.partition_broadcast(B)))
        cond_sb = sb("cond_sb", [B, C])
        loads.append((cond_sb[:], cond))

        ident = sb("ident", [P, P])
        identb = sb("identb", [P, P], BF16)
        negbig = sb("negbig", [P, P], BF16)
        ones2 = sb("ones2", [P, 2, 2 * D])
        neg_half = sb("neg_half", [P, 4])
        zero_col = sb("zero_col", [P, 1])
        cond_t = sb("cond_t", [B, C])
        silu_c = sb("silu_c", [B, C])
        silu_T = sb("silu_T", [P, NC, B])
        bias_col = sb("bias_col", [P, NROW])
        half_col = sb("half_col", [P, 2 * NJ])
        q_col = sb("q_col", [P, 3, NC])
        mod = sb("mod", [P, B, 2 * NC * 5])
        gates = prob[0:B].rearrange("b s n -> b (s n)")[:, 0:6 * C].rearrange("b (g c) -> b g c", g=6)
        x_sb = sb("x_sb", [P, NT, C])
        c_sb = sb("c_sb", [P, NT, C])
        gate_sb = sb("gate_sb", [P, 6, C])
        mod_b = sb("mod_b", [P, 2 * NC * 5])
        stats = sb("stats", [P, 4, 6])
        mv = sb("mv", [P, 4, 2])
        var_eps = sb("var_eps", [P, 4])
        rstd = sb("rstd", [P, 4])
        xn = sb("xn", [P, 4, C])
        xT = sb("xT", [P, NC, L])
        cT = sb("cT", [P, NC, L])
        rT = sb("rT", [P, NC, L])
        hT = sb("hT", [P, NC, L])
        parts = sb("parts", [P, 2, NPART, NC, L], BF16)
        TQ = [sb(f"TQ{a}", [P, H, L], BF16) for a in range(2)]
        TK = [sb(f"TK{a}", [P, H, L], BF16) for a in range(2)]
        TQ, TK = [TQ[0], TQ[0], TQ[1]], [TK[0], TK[0], TK[1]]
        V = [sb(f"V{a}", [P, NT, H * 2 * D]) for a in range(3)]
        mx = [sb(f"mx{a}", [P, NT, H]) for a in range(2)]
        top1 = sb("top1", [P, NT, H, 8])
        top2 = sb("top2", [P, 2, 2, 8])
        left = sb("left", [P, 2, 2, L])
        negm = sb("negm", [P, 3, 2, NT, H], BF16)
        negmT = sb("negmT", [2 * NT * H, 3, P], BF16)
        rsum = sb("rsum", [P, 2, L])
        ON = [sb(f"ON{a}", [P, NC, L]) for a in range(3)]
        res = [sb(f"res{i}", [P, NT, C]) for i in range(4)]
        base = sb("base", [P, NT, C])
        gated = sb("gated", [P, NT, C])
        th = sb("th", [P, 2, L])
        ub = sb("ub", [P, 2, L])
        uw = sb("uw", [P, 2, L])

        pj = [ctx.enter_context(nc.psum_tensor(f"pj{i}", [P, 512], F32)) for i in range(2)]
        ps = [ctx.enter_context(nc.psum_tensor(f"ps{i}", [P, 512], F32)) for i in range(2)]
        pt = [ctx.enter_context(nc.psum_tensor(f"pt{i}", [P, 512], F32)) for i in range(2)]
        po = [ctx.enter_context(nc.psum_tensor(f"po{i}", [P, 512], F32)) for i in range(2)]

        w_in = sem("w_in")
        setup_pool = sem("setup_pool")
        setup_act = sem("setup_act")
        setup_pe = sem("setup_pe")
        setup_dve = sem("setup_dve")
        gates_out = sem("gates_out")
        settled = [sem("settled"), sem("settled_sp")]
        NPJ = len(PJ) // 2
        OD_UNITS = [NS // 2, NS, NS + NW * H // 8, NS + NW * H // 4,
                    NS + NW * H // 4 + NS // 2, 2 * NS + NW * H // 4]
        pj_full = [signal(f"pj_full{i}", NPJ) for i in range(2)]
        pj_free = [signal(f"pj_free{i}", NPJ, 1) for i in range(2)]
        NSU = 2 * NS + NW * H // 4
        s_full = signal("s_full", NSU)
        s_free = signal("s_free", NSU, 2)
        NEU = 2 * NS + NW * H // 4
        st_full = signal("st_full", NEU)
        e_done = signal("e_done", NEU, 2)
        pv_done = signal("pv_done", NEU, 4)
        od_free = signal("od_free", 6, 2)
        x_in = signal("x_in", 1, 0, 32)
        gate_in = signal("gate_in", 1, 0, 16)
        ln_stats = signal("ln_stats", 4)
        ln_rstd = signal("ln_rstd", 4)
        xn_ready = signal("xn_ready", 4)
        xt_ready = signal("xt_ready", 6)
        f_ready = signal("f_ready", 6)
        p1_ready = signal("p1_ready", 6)
        r_ready = signal("r_ready", 6)
        p2_ready = signal("p2_ready", 6)
        p3_ready = signal("p3_ready", 6)
        parts_out = {t: signal(f"parts_out_{t}", 1, 1, 16) for t in TENSORS}
        parts_in = {t: signal(f"parts_in_{t}", 6, 6, 16) for t in TENSORS}
        v_ready = [signal(f"v_ready{a}", 1) for a in range(3)]
        negm_ready = signal("negm_ready", 3)
        negmT_ready = signal("negmT_ready", 3)
        m_in = [signal(f"m_in{a}", 2 * NT, 0, 16) for a in range(3)]
        left_ready = signal("left_ready", NS)
        other_ready = signal("other_ready", NS, 2)
        on_ready = signal("on_ready", 6, 6)
        base_ready = signal("base_ready", 4, 4)
        gated_ready = signal("gated_ready", 3)
        res_ready = signal("res_ready", 4)
        mod_ready = signal("mod_ready", 1)
        t_ready = signal("t_ready", NJ)
        h_ready = signal("h_ready", NJ, 2)
        y_out = signal("y_out", 1, 1, 16)
        xt_all = signal("xt_all", 1, 1)
        pool_step = signal("pool_step", 4)
        act_step = signal("act_step", ACT_STEPS)
        dve_step = signal("dve_step", DVE_STEPS)

        def need(eng, *waits, settle=False):
            vals = [(s, v if isinstance(v, int) else eng.snap(v)) for s, v in waits]
            for n, (s, v) in enumerate(vals):
                eng.wait_ge(s, v)
                if eng is SP[0] or settle and n == len(vals) - 1:
                    eng.sem_inc(settled[eng is SP[0]], 1)

        def pj_slot(name):
            n = PJ.index(name)
            return n % 2, n // 2

        LN_SRC = [x_sb, res[0], res[1], res[2]]

        block = ctx.enter_context(nc.Block())

        SP = [None]

        @block.sync
        def _(sp):
            SP[0] = sp
            for dst, src in loads:
                sp.dma_start(dst, src).then_inc(w_in, 16)
            sp.wait_ge(setup_dve, SETUP_DVE_GATES)
            sp.dma_start(gates_dram, gates.rearrange("b g c -> b (g c)")).then_inc(gates_out, 16)
            sp.wait_ge(gates_out, 16)

            def bounce(b, t):
                a, isq = int(t[1]), t[0] == "q"
                n = TENSORS.index(t)
                need(sp, (p3_ready.sem, p3_ready.at(b, n + 1)),
                     (parts_in[t].sem, parts_in[t].before(b, 6)))
                sp.dma_start(parts_dram[t].rearrange("i (m p) n -> p i m n", p=P), parts[:, n % 2]
                             ).then_inc(parts_out[t].sem, 16)
                need(sp, (parts_out[t].sem, parts_out[t].at(b, 1)),
                     (on_ready.sem, on_ready.before(b, 2 * a + 2)))
                for i, part in enumerate(Q_PARTS if isq else K_PARTS):
                    dst = (TQ if isq else TK)[a]
                    sp.dma_start(dst[i * D:(i + 1) * D, :, :],
                                 parts_dram[t][part].rearrange("(h d) n -> d h n", d=D)).then_inc(parts_in[t].sem, 16)

            def max_rows(b, a):
                need(sp, (negmT_ready.sem, negmT_ready.at(b, a + 1)))
                for i in range(2):
                    for qt in range(NT):
                        r = (i * NT + qt) * H
                        sp.dma_start(TQ[a][KP + i:KP + i + 1, :, qt * P:(qt + 1) * P],
                                     negmT[r:r + H, a, :]).then_inc(m_in[a].sem, 16)

            with sp.Fori(0, B) as b:
                need(sp, (base_ready.sem, base_ready.before(b, 4)),
                     (on_ready.sem, on_ready.before(b, 2)))
                sp.dma_start(x_sb[:], x[b].rearrange("(t p) c -> p t c", p=P)).then_inc(x_in.sem, 16)
                sp.dma_start(c_sb[:], ctx_in[b].rearrange("(t p) c -> p t c", p=P)).then_inc(x_in.sem, 16)
                sp.dma_start(gate_sb[:].rearrange("p g c -> p (g c)"), gates_dram[b].partition_broadcast(P)
                             ).then_inc(gate_in.sem, 16)
                for t in ("q0", "k0", "k2"):
                    bounce(b, t)
                max_rows(b, CROSS)
                for t in ("q1", "k1"):
                    bounce(b, t)
                max_rows(b, SELF)
                bounce(b, "q2")
                max_rows(b, TOPK)
                need(sp, (res_ready.sem, res_ready.at(b, 4)))
                sp.dma_start(out[b].rearrange("(t p) c -> p t c", p=P), res[3][:]).then_inc(y_out.sem, 16)
            sp.wait_ge(y_out.sem, 16 * (B + 1))
            for t in TENSORS:
                sp.wait_ge(parts_out[t].sem, 16 * (B + 1))

        @block.gpsimd
        def _(pool):
            pool.memset(ident[:], 0.0).then_inc(setup_pool, 1)
            pool.wait_ge(setup_pool, 1)
            pool.affine_select(out=ident[:], in_=ident[:], compare_op=ALU.not_equal, fill=1.0, base=0,
                               pattern=[[-1, P]], channel_multiplier=1).then_inc(setup_pool, 1)
            pool.memset(neg_half[:], -0.5).then_inc(setup_pool, 1)
            pool.memset(ones2[:], 0.0).then_inc(setup_pool, 1)
            pool.wait_ge(setup_pool, 4)
            pool.memset(ones2[:, 0, 0:D], 1.0).then_inc(setup_pool, 1)
            pool.memset(ones2[:, 1, D:2 * D], 1.0).then_inc(setup_pool, 1)
            for a in range(3):
                pool.memset(V[a][:], 0.0).then_inc(setup_pool, 1)
            for a in (CROSS, TOPK):
                pool.wait_ge(setup_pool, SETUP_POOL - 2 + (a == TOPK))
                pool.memset(TK[a][KP:KM, :, :], 1.0).then_inc(setup_pool, 1)
            pool.wait_ge(setup_pool, SETUP_POOL)
            for s in seeds:
                pool.sem_inc(s.sem, s.seed * s.unit)
            pool.wait_ge(setup_dve, SETUP_DVE)

            def rstd_of(b, n, tiles, eps):
                need(pool, (ln_stats.sem, ln_stats.at(b, n + 1)), settle=True)
                pool.tensor_scalar(var_eps[:, 0:tiles], mv[:, 0:tiles, 1], eps, None, ALU.add).then_inc(pool_step.sem, 1)
                k = pool_k()
                need(pool, (pool_step.sem, pool_step.at(b, k)))
                pool.tensor_tensor(rstd[:, 0:tiles], var_eps[:, 0:tiles], neg_half[:, 0:tiles], ALU.pow
                                   ).then_inc(ln_rstd.sem, 1)

            def split(b, t):
                n = TENSORS.index(t)
                s = n % 2
                need(pool, (p1_ready.sem, p1_ready.at(b, n + 1)))
                pool.tensor_tensor(rest[:, s], full[:, s], parts[:, s, 0], ALU.subtract).then_inc(r_ready.sem, 1)
                need(pool, (p2_ready.sem, p2_ready.at(b, n + 1)))
                pool.tensor_tensor(parts[:, s, 2], rest[:, s], parts[:, s, 1], ALU.subtract).then_inc(p3_ready.sem, 1)

            count = [0]

            def pool_k():
                count[0] += 1
                return count[0]

            with pool.Fori(0, B) as b:
                count[0] = 0
                need(pool, (base_ready.sem, base_ready.before(b, 4)), (xt_all.sem, xt_all.before(b, 1)))
                pool.tensor_copy(mod_b[:], mod[:, bass.ds(b, 1), :].rearrange("p o m -> p (o m)")).then_inc(mod_ready.sem, 1)
                rstd_of(b, 0, 4, 1e-5)
                for t in ("q0", "k0", "k2"):
                    split(b, t)
                need(pool, (x_in.sem, x_in.at(b, 1)))
                for t in range(NT):
                    ins = pool.tensor_tensor(base[:, t, :], x_sb[:, t, :], vb[:, 3, :], ALU.add)
                ins.then_inc(base_ready.sem, 1)
                for i, eps in ((1, 1e-6), (2, 1e-6), (3, 1e-6)):
                    rstd_of(b, i, 2, eps)
                    for t in (("q1", "k1"), ("q2",), ())[i - 1]:
                        split(b, t)
                    need(pool, (gate_in.sem, gate_in.at(b, 1)), (res_ready.sem, res_ready.at(b, i)))
                    for t in range(NT):
                        ins = pool.tensor_tensor(base[:, t, :], res[i - 1][:, t, :], gate_sb[:, 2 + i, :], ALU.add)
                    ins.then_inc(base_ready.sem, 1)
                    waits = [(base_ready.sem, base_ready.at(b, i + 1)), (gated_ready.sem, gated_ready.at(b, i))]
                    if i == 3:
                        waits.append((y_out.sem, y_out.before(b, 1)))
                    need(pool, *waits)
                    pool.tensor_tensor(res[i][:], base[:], gated[:], ALU.add).then_inc(res_ready.sem, 1)
            assert count[0] == pool_step.per

        @block.tensor
        def _(pe):
            pe.wait_ge(w_in, 16 * len(loads))
            pe.wait_ge(setup_pool, SETUP_POOL)
            pe.wait_ge(setup_dve, 2)
            pe.transpose(ps[0][:, 0:NROW], bias_rows[:], ident[0:NROW, 0:NROW])
            for c in range(NC):
                ins = pe.transpose(ps[1][:, c * B:(c + 1) * B], silu_c[:, c * P:(c + 1) * P], ident[0:B, 0:B])
            ins.then_inc(setup_pe, 1)
            pe.wait_ge(setup_act, 3)
            wmod = [W["wss0"], W["wss1"], W["ada"]]
            for m, (w, o, _) in enumerate(MODS):
                for c in range(NC):
                    for k in range(NC):
                        pe.matmul(po[0][:, (m * NC + c) * B:(m * NC + c + 1) * B],
                                  wmod[w][:, k, o + c * P:o + (c + 1) * P], silu_T[:, k, :],
                                  start=(k == 0), stop=(k == NC - 1))
            for i, g in enumerate((2, 5, 8)):
                dst = pt[i // 2][0:B, (i % 2) * C:(i % 2 + 1) * C]
                for k in range(NC):
                    ins = pe.matmul(dst, silu_T[:, k, :], W["ada"][:, k, g * C:(g + 1) * C],
                                    start=(k == 0), stop=(k == NC - 1))
            ins.then_inc(setup_pe, 1)
            pe.wait_ge(setup_dve, SETUP_DVE)

            def pj_begin(b, name, *waits, settle=False):
                i, k = pj_slot(name)
                need(pe, (pj_free[i].sem, pj_free[i].room(b, k)), *waits, settle=settle)
                return pj[i]

            def pj_end(name, ins):
                ins.then_inc(pj_full[pj_slot(name)[0]].sem, 1)

            def transpose_in(b, name, src, o, *waits):
                bank = pj_begin(b, name, *waits)
                for c in range(NC):
                    for t in range(NT):
                        ins = pe.transpose(bank[:, c * L + t * P:c * L + (t + 1) * P],
                                           src[:, o + t, c * P:(c + 1) * P], ident[:])
                pj_end(name, ins)

            def project_T(b, name, w, col, src, *waits):
                bank = pj_begin(b, name, *waits)
                for m in range(NC):
                    for k in range(NC):
                        ins = pe.matmul(bank[:, m * L:(m + 1) * L], w[:, k, col + m * P:col + (m + 1) * P],
                                        src[:, k, :], start=(k == 0), stop=(k == NC - 1))
                pj_end(name, ins)

            def project(b, name, w, col, src, nk, *waits):
                bank = pj_begin(b, name, *waits)
                for t in range(NT):
                    for k in range(nk):
                        ins = pe.matmul(bank[:, t * C:(t + 1) * C], src[:, k, t * P:(t + 1) * P],
                                        w[:, k, col:col + C], start=(k == 0), stop=(k == nk - 1))
                pj_end(name, ins)

            unit_s = [0]

            def scores(b, a):
                need(pe, (parts_in[f"q{a}"].sem, parts_in[f"q{a}"].at(b, 6)),
                     (parts_in[f"k{a}"].sem, parts_in[f"k{a}"].at(b, 6)))
                n = L if a != SELF else WIN
                per = 512 // n
                for hp in range(H // per):
                    for qt in range(NT):
                        u = unit_s[0]
                        unit_s[0] += 1
                        need(pe, (s_free.sem, s_free.room(b, u)))
                        for i in range(per):
                            h = hp * per + i
                            k0 = 0 if a != SELF else qt * WIN
                            ins = pe.matmul(ps[u % 2][:, i * n:(i + 1) * n], TQ[a][0:KP, h, qt * P:(qt + 1) * P],
                                            TK[a][0:KP, h, k0:k0 + n], start=True, stop=True)
                        ins.then_inc(s_full.sem, 1)

            def max_T(b, a):
                name = f"mt{a}"
                bank = pj_begin(b, name, (negm_ready.sem, negm_ready.at(b, a + 1)), settle=True)
                rows = 2 * NT * H
                pj_end(name, pe.transpose(bank[0:rows, 0:P // 2].bitcast(BF16),
                                          negm[:, a].rearrange("p i t h -> p (i t h)"), identb[:]))

            unit_e = [0]

            def units(a):
                out = []
                for hh in range(NC):
                    for kb in range(NT):
                        for par in range(2):
                            heads = [2 * j + par for j in range(HH // 2)]
                            if a == SELF:
                                out.append((hh, kb, heads))
                            else:
                                out += [(hh, kb, heads[0:2]), (hh, kb, heads[2:4])]
                return out

            def attend(b, a):
                us = units(a)
                u0 = unit_e[0]
                unit_e[0] += len(us)
                need(pe, (m_in[a].sem, m_in[a].at(b, 2 * NT)))
                nq = L if a != SELF else WIN
                if a == TOPK:
                    need(pe, (other_ready.sem, other_ready.at(b, NS)))
                need(pe, (v_ready[a].sem, v_ready[a].at(b, 1)))

                def scores_T(n):
                    hh, kb, heads = us[n]
                    u = u0 + n
                    need(pe, (e_done.sem, e_done.room(b, u)))
                    for i, h8 in enumerate(heads):
                        h = hh * HH + h8
                        q0 = 0 if a != SELF else kb * WIN
                        dst = pt[u % 2][:, i * nq:(i + 1) * nq]
                        ins = pe.matmul(dst, TK[a][0:KM, h, kb * P:(kb + 1) * P], TQ[a][0:KM, h, q0:q0 + nq],
                                        start=True, stop=True)
                        if a == TOPK:
                            for qt in range(NT):
                                ins = pe.matmul(pt[u % 2][:, i * nq + qt * P:i * nq + (qt + 1) * P],
                                                other[:, qt, h, kb * P:(kb + 1) * P], negbig[:],
                                                start=False, stop=True, skip_group_check=True)
                    ins.then_inc(st_full.sem, 1)

                seen = set()

                def values(ns):
                    ins = None
                    hh = us[ns[0]][0]
                    waits = [(e_done.sem, e_done.at(b, u0 + ns[-1] + 1))]
                    if (hh, "wait") not in seen:
                        seen.add((hh, "wait"))
                        waits.append((od_free.sem, od_free.room(b, 2 * a + hh)))
                    need(pe, *waits)
                    for what in range(2):
                        for n in ns:
                            hh, kb, heads = us[n]
                            od = 2 * a + hh
                            q0 = 0 if a != SELF else kb * WIN
                            last = n == len(us) - 1 or us[n + 1][0] != hh
                            for i, h8 in enumerate(heads):
                                h = hh * HH + h8
                                j = h8 // 2
                                w = ones2[:, h8 % 2, :] if what else V[a][:, kb, h * 2 * D:(h + 1) * 2 * D]
                                first = (hh, j) not in seen
                                seen.add((hh, j))
                                ins = pe.matmul(po[od % 2][32 * j:32 * j + 32, what * L + q0:what * L + q0 + nq], w,
                                                prob[:, (u0 + n) % 4, i * nq:(i + 1) * nq],
                                                start=first, stop=True, skip_group_check=True)
                            if what:
                                ins.then_inc(pv_done.sem, 1)

                scores_T(0)
                scores_T(1)
                for g in range(len(us) // 2):
                    if g + 1 < len(us) // 2:
                        scores_T(2 * g + 2)
                        scores_T(2 * g + 3)
                    values([2 * g, 2 * g + 1])

            with pe.Fori(0, B) as b:
                unit_s[0] = unit_e[0] = 0
                transpose_in(b, "tx", xn, 0, (xn_ready.sem, xn_ready.at(b, 1)))
                transpose_in(b, "tc", xn, 2)
                transpose_in(b, "tr", c_sb, 0, (x_in.sem, x_in.at(b, 1)))
                project_T(b, "q0", W["q0"], 0, xT, (xt_ready.sem, xt_ready.at(b, 1)))
                project_T(b, "k0", W["kv0"], 0, cT, (xt_ready.sem, xt_ready.at(b, 2)))
                project(b, "v0", W["kv0"], C, cT, NC)
                project_T(b, "k2", W["kv2"], 0, rT, (xt_ready.sem, xt_ready.at(b, 3)))
                project(b, "v2", W["kv2"], C, rT, NC)
                scores(b, CROSS)
                max_T(b, CROSS)
                attend(b, CROSS)
                project(b, "o0", W["p0"], 0, ON[CROSS], NC, (on_ready.sem, on_ready.at(b, 2)))
                transpose_in(b, "th1", xn, 0, (xn_ready.sem, xn_ready.at(b, 2)))
                project_T(b, "q1", W["qkv1"], 0, hT, (xt_ready.sem, xt_ready.at(b, 4)))
                project_T(b, "k1", W["qkv1"], C, hT)
                project(b, "v1", W["qkv1"], 2 * C, hT, NC)
                scores(b, SELF)
                max_T(b, SELF)
                attend(b, SELF)
                project(b, "o1", W["p1"], 0, ON[SELF], NC, (on_ready.sem, on_ready.at(b, 4)))
                transpose_in(b, "th2", xn, 0, (xn_ready.sem, xn_ready.at(b, 3)))
                project_T(b, "q2", W["q2"], 0, hT, (xt_ready.sem, xt_ready.at(b, 5)))
                scores(b, TOPK)
                max_T(b, TOPK)
                attend(b, TOPK)
                project(b, "o2", W["p2"], 0, ON[TOPK], NC, (on_ready.sem, on_ready.at(b, 6)))
                transpose_in(b, "th3", xn, 0, (xn_ready.sem, xn_ready.at(b, 4)))
                need(pe, (xt_ready.sem, xt_ready.at(b, 6)))
                for j in range(NJ):
                    bank = pj_begin(b, f"h{j}")
                    for half in range(2):
                        for k in range(NC):
                            ins = pe.matmul(bank[:, half * L:(half + 1) * L],
                                            W["m1"][:, k, half * HID + j * P:half * HID + (j + 1) * P],
                                            hT[:, k, :], start=(k == 0), stop=(k == NC - 1))
                    pj_end(f"h{j}", ins)
                project(b, "o3", W["m2"], 0, hid, NJ, (h_ready.sem, h_ready.at(b, NJ)))

        @block.scalar
        def _(act):
            act.wait_ge(w_in, 16 * len(loads))
            act.activation(cond_t[:], cond_sb[:], ACT.Tanh, scale=0.5).then_inc(setup_act, 1)
            act.wait_ge(setup_pe, 1)
            act.activation(bias_col[:], ps[0][:, 0:NROW], ACT.Copy).then_inc(setup_act, 1)
            act.activation(silu_T[:].rearrange("p c b -> p (c b)"), ps[1][:, 0:NC * B], ACT.Copy).then_inc(setup_act, 1)
            act.wait_ge(setup_dve, SETUP_DVE)

            def pj_wait(b, name, *waits):
                i, k = pj_slot(name)
                need(act, (pj_full[i].sem, pj_full[i].at(b, k + 1)), *waits)
                return pj[i]

            def modulated(b, name, dst, m, roll, *waits):
                bank = pj_wait(b, name, *waits)
                for c in range(NC):
                    kw = {} if m is None else dict(scale=mod_b[:, m * NC + c:m * NC + c + 1],
                                                   bias=mod_b[:, (m + 1) * NC + c:(m + 1) * NC + c + 1])
                    pieces = ((0, L, 0),) if not roll else ((SHIFT, L, 0), (0, SHIFT, L - SHIFT))
                    for lo, hi, to in pieces:
                        ins = act.activation(dst[:, c, to:to + hi - lo], bank[:, c * L + lo:c * L + hi],
                                             ACT.Identity if m is not None else ACT.Copy, **kw)
                        ins.then_inc(act_step.sem, 1)
                        act_count[0] += 1
                need(act, (act_step.sem, act_step.at(b, act_count[0])))
                act.sem_inc(xt_ready.sem, 1)
                act.sem_inc(pj_free[pj_slot(name)[0]].sem, 1)

            act_count = [0]

            def full_of(b, t):
                n = TENSORS.index(t)
                a = int(t[1])
                waits = []
                if n >= 2:
                    p = TENSORS[n - 2]
                    waits.append((parts_out[p].sem, parts_out[p].at(b, 1)))
                else:
                    p = TENSORS[len(TENSORS) - 2 + n]
                    waits.append((parts_out[p].sem, parts_out[p].before(b, 1)))
                bank = pj_wait(b, t, *waits)
                for m in range(NC):
                    if t[0] == "q":
                        kw = dict(scale=SCALE, bias=q_col[:, a, m:m + 1])
                    else:
                        r = (R_K0, R_QK1 + NC, R_K2)[a] + m
                        kw = dict(bias=bias_col[:, r:r + 1])
                    act.activation(full[:, n % 2, m, :], bank[:, m * L:(m + 1) * L], ACT.Identity, **kw
                                   ).then_inc(act_step.sem, 1)
                    act_count[0] += 1
                need(act, (act_step.sem, act_step.at(b, act_count[0])))
                act.sem_inc(f_ready.sem, 1)
                act.sem_inc(pj_free[pj_slot(t)[0]].sem, 1)

            def max_T(b, a):
                name = f"mt{a}"
                bank = pj_wait(b, name)
                rows = 2 * NT * H
                act.activation(negmT[:, a, :], bank[0:rows, 0:P // 2].bitcast(BF16), ACT.Copy
                               ).then_inc(act_step.sem, 1)
                act_count[0] += 1
                need(act, (act_step.sem, act_step.at(b, act_count[0])))
                act.sem_inc(negmT_ready.sem, 1)
                act.sem_inc(pj_free[pj_slot(name)[0]].sem, 1)

            unit_e = [0]

            def exps(b, a):
                n = 2 * H // 2 if a != SELF else NW * H // 4
                for u in range(unit_e[0], unit_e[0] + n):
                    need(act, (st_full.sem, st_full.at(b, u + 1)), (pv_done.sem, pv_done.room(b, u)))
                    act.activation(prob[:, u % 4, :], pt[u % 2][:], ACT.Exp).then_inc(e_done.sem, 1)
                unit_e[0] += n

            with act.Fori(0, B) as b:
                unit_e[0] = act_count[0] = 0
                modulated(b, "tx", xT, M_XQ, False, (mod_ready.sem, mod_ready.at(b, 1)))
                modulated(b, "tc", cT, M_XKV, False)
                modulated(b, "tr", rT, None, False)
                for t in ("q0", "k0", "k2"):
                    full_of(b, t)
                max_T(b, CROSS)
                exps(b, CROSS)
                modulated(b, "th1", hT, M_MSA, True)
                for t in ("q1", "k1"):
                    full_of(b, t)
                max_T(b, SELF)
                exps(b, SELF)
                modulated(b, "th2", hT, M_MCA, False)
                full_of(b, "q2")
                for u in range(NS):
                    need(act, (left_ready.sem, left_ready.at(b, u + 1)))
                    hp, qt = u // NT, u % NT
                    act.activation(other[:, qt, 2 * hp:2 * hp + 2, :], left[:, u % 2], ACT.Relu,
                                   bias=1.0, scale=1.0 / BIG).then_inc(other_ready.sem, 1)
                max_T(b, TOPK)
                exps(b, TOPK)
                modulated(b, "th3", hT, M_MLP, False)
                act.sem_inc(xt_all.sem, 1)
                for j in range(NJ):
                    s = j % 2
                    bank = pj_wait(b, f"h{j}", (h_ready.sem, h_ready.room(b, j)))
                    act.activation(th[:, s, :], bank[:, 0:L], ACT.Tanh, scale=0.5,
                                   bias=half_col[:, j:j + 1]).then_inc(act_step.sem, 1)
                    act_count[0] += 1
                    act.activation(ub[:, s, :], bank[:, L:2 * L], ACT.Identity, scale=0.5,
                                   bias=half_col[:, NJ + j:NJ + j + 1]).then_inc(t_ready.sem, 1)
            assert act_count[0] == act_step.per, act_count

        @block.vector
        def _(dve):
            done = [0]

            def setup(ins):
                done[0] += 1
                ins.then_inc(setup_dve, 1)
                dve.wait_ge(setup_dve, done[0])

            dve.wait_ge(setup_act, 1)
            setup(dve.scalar_tensor_tensor(out=silu_c[:], in0=cond_t[:], scalar=1.0, in1=cond_sb[:],
                                           op0=ALU.add, op1=ALU.mult))
            setup(dve.tensor_scalar(silu_c[:], silu_c[:], 0.5, None, ALU.mult))
            dve.wait_ge(setup_pool, SETUP_POOL)
            setup(dve.tensor_copy(identb[:], ident[:]))
            setup(dve.tensor_scalar(negbig[:], ident[:], -BIG, None, ALU.mult))
            dve.wait_ge(setup_act, 3)
            dve.wait_ge(setup_pe, 2)
            for a, r in enumerate((R_Q0, R_QK1, R_Q2)):
                setup(dve.tensor_scalar(q_col[:, a, :], bias_col[:, r:r + NC], SCALE, None, ALU.mult))
            setup(dve.tensor_scalar(half_col[:], bias_col[:, R_M1:R_M1 + 2 * NJ], 0.5, None, ALU.mult))
            for m, (w, o, one) in enumerate(MODS):
                for c in range(NC):
                    r = (R_SSQ, R_SSKV, R_ADA)[w] + o // P + c
                    i = m * NC + c
                    setup(dve.tensor_scalar(mod[:, :, i], po[0][:, i * B:(i + 1) * B], bias_col[:, r:r + 1],
                                            float(one), ALU.add, ALU.add))
            for i in range(3):
                setup(dve.tensor_tensor(gates[:, i, :], pt[i // 2][0:B, (i % 2) * C:(i % 2 + 1) * C],
                                        gate_bias[:, i, :], ALU.add))
                setup(dve.tensor_tensor(gates[:, 3 + i, :], gates[:, i, :], gate_bias[:, 3 + i, :], ALU.mult))
            assert done[0] == SETUP_DVE_GATES
            setup(dve.memset(zero_col[:], 0.0))
            assert done[0] == SETUP_DVE

            count = [0]

            def step(ins):
                ins.then_inc(dve_step.sem, 1)
                count[0] += 1
                return count[0]

            def after(b, k, settle=False):
                need(dve, (dve_step.sem, dve_step.at(b, k)), settle=settle)

            def pj_wait(b, name, *waits):
                i, k = pj_slot(name)
                need(dve, (pj_full[i].sem, pj_full[i].at(b, k + 1)), *waits)
                return pj[i], pj_free[i].sem

            def layernorm(b, n, tiles):
                for i, t in enumerate(tiles):
                    k = step(dve.bn_stats(stats[:, i, :], t))
                after(b, k, settle=True)
                for i in range(len(tiles)):
                    ins = dve.bn_aggr(mv[:, i, :], stats[:, i, :])
                ins.then_inc(ln_stats.sem, 1)
                need(dve, (ln_rstd.sem, ln_rstd.at(b, n + 1)))
                for i, t in enumerate(tiles):
                    ins = dve.tensor_scalar(xn[:, i, :], t, mv[:, i, 0:1], rstd[:, i:i + 1], ALU.subtract, ALU.mult)
                ins.then_inc(xn_ready.sem, 1)

            def split(b, t):
                n = TENSORS.index(t)
                s = n % 2
                need(dve, (f_ready.sem, f_ready.at(b, n + 1)))
                dve.tensor_copy(parts[:, s, 0], full[:, s]).then_inc(p1_ready.sem, 1)
                need(dve, (r_ready.sem, r_ready.at(b, n + 1)))
                dve.tensor_copy(parts[:, s, 1], rest[:, s]).then_inc(p2_ready.sem, 1)

            def values(b, a):
                bank, free = pj_wait(b, f"v{a}")
                for t in range(NT):
                    dst = V[a][:, t, :].rearrange("p (j i d) -> p j i d", i=4, d=D)[:, :, 0:4:3, :]
                    src = bank[:, t * C:(t + 1) * C].rearrange("p (j i d) -> p j i d", i=2, d=D)
                    bias = vb[:, a, :].rearrange("p (j i d) -> p j i d", i=2, d=D)
                    k = step(dve.tensor_tensor(dst, src, bias, ALU.add))
                after(b, k)
                dve.sem_inc(v_ready[a].sem, 1)
                dve.sem_inc(free, 1)

            unit_s = [0]

            def negate_max(b, a, m, k):
                after(b, k)
                k = step(dve.tensor_scalar(negm[:, a, 0], m, -1.0, None, ALU.mult))
                after(b, k)
                dve.scalar_tensor_tensor(out=negm[:, a, 1], in0=m, scalar=-1.0, in1=negm[:, a, 0],
                                         op0=ALU.mult, op1=ALU.subtract).then_inc(negm_ready.sem, 1)

            def maxima(b, a):
                n = L if a == CROSS else WIN
                per = 512 // n
                for hp in range(H // per):
                    for qt in range(NT):
                        u = unit_s[0]
                        unit_s[0] += 1
                        need(dve, (s_full.sem, s_full.at(b, u + 1)))
                        dve.tensor_reduce(mx[a][:, qt, hp * per:(hp + 1) * per],
                                          ps[u % 2][:].rearrange("p (h n) -> p h n", n=n), AX_X, ALU.max
                                          ).then_inc(s_free.sem, 1)
                need(dve, (s_free.sem, s_free.at(b, unit_s[0])))
                negate_max(b, a, mx[a][:], count[0])

            def top16(b):
                for u in range(NS):
                    g = unit_s[0]
                    unit_s[0] += 1
                    hp, qt = u // NT, u % NT
                    need(dve, (s_full.sem, s_full.at(b, g + 1)), (other_ready.sem, other_ready.room(b, u)), settle=True)
                    src = [ps[g % 2][:, i * L:(i + 1) * L] for i in range(2)]
                    lft = [left[:, u % 2, i, :] for i in range(2)]
                    t1 = [top1[:, qt, 2 * hp + i, :] for i in range(2)]
                    t2 = [top2[:, u % 2, i, :] for i in range(2)]
                    ks = [step(dve.max(t1[i], src[i])) for i in range(2)]
                    for i in range(2):
                        after(b, ks[i], settle=True)
                        ks[i] = step(dve.match_replace(lft[i], t1[i], src[i], -2 * BIG))
                    for i in range(2):
                        after(b, ks[i], settle=True)
                        ks[i] = step(dve.max(t2[i], lft[i]))
                    dve.sem_inc(s_free.sem, 1)
                    for i in range(2):
                        after(b, ks[i], settle=True)
                        ks[i] = step(dve.match_replace(lft[i], t2[i], lft[i], -2 * BIG))
                    after(b, ks[1])
                    dve.sem_inc(left_ready.sem, 1)
                negate_max(b, TOPK, top1[:, :, :, 0], count[0])

            def normalise(b, a):
                for hh in range(NC):
                    od = 2 * a + hh
                    need(dve, (pv_done.sem, pv_done.at(b, OD_UNITS[od])))
                    k = step(dve.reciprocal(rsum[:, hh, :], po[od % 2][:, L:2 * L]))
                    after(b, k)
                    pieces = ((0, L, 0),) if a != SELF else ((0, L - SHIFT, SHIFT), (L - SHIFT, L, 0))
                    for lo, hi, to in pieces:
                        k = step(dve.tensor_tensor(ON[a][:, hh, to:to + hi - lo], po[od % 2][:, lo:hi],
                                                   rsum[:, hh, lo:hi], ALU.mult))
                    after(b, k)
                    dve.sem_inc(on_ready.sem, 1)
                    dve.sem_inc(od_free.sem, 1)

            def tiles(src):
                return [src[:, t, :] for t in range(NT)]

            with dve.Fori(0, B) as b:
                count[0] = unit_s[0] = 0
                need(dve, (x_in.sem, x_in.at(b, 1)))
                layernorm(b, 0, tiles(x_sb) + tiles(c_sb))
                split(b, "q0")
                split(b, "k0")
                values(b, CROSS)
                split(b, "k2")
                values(b, TOPK)
                maxima(b, CROSS)
                normalise(b, CROSS)
                bank, free = pj_wait(b, "o0", (base_ready.sem, base_ready.at(b, 1)))
                k = step(dve.tensor_tensor(res[0][:].rearrange("p t c -> p (t c)"), bank[:],
                                           base[:].rearrange("p t c -> p (t c)"), ALU.add))
                after(b, k)
                dve.sem_inc(res_ready.sem, 1)
                dve.sem_inc(free, 1)
                for i in (1, 2, 3):
                    need(dve, (res_ready.sem, res_ready.at(b, i)))
                    layernorm(b, i, tiles(res[i - 1]))
                    if i == 1:
                        split(b, "q1")
                        split(b, "k1")
                        values(b, SELF)
                        maxima(b, SELF)
                        normalise(b, SELF)
                    if i == 2:
                        split(b, "q2")
                        top16(b)
                        normalise(b, TOPK)
                    if i == 3:
                        for j in range(NJ):
                            s = j % 2
                            bank, free = pj_wait(b, f"h{j}", (t_ready.sem, t_ready.at(b, j + 1)))
                            k = step(dve.scalar_tensor_tensor(out=uw[:, s, :], in0=bank[:, 0:L],
                                                              scalar=bias_col[:, R_M1 + j:R_M1 + j + 1],
                                                              in1=ub[:, s, :], op0=ALU.add, op1=ALU.mult))
                            after(b, k)
                            dve.sem_inc(free, 1)
                            dve.scalar_tensor_tensor(out=hid[:, j, :], in0=th[:, s, :], scalar=1.0, in1=uw[:, s, :],
                                                     op0=ALU.add, op1=ALU.mult).then_inc(h_ready.sem, 1)
                    bank, free = pj_wait(b, f"o{i}", (gate_in.sem, gate_in.at(b, 1)))
                    for t in range(NT):
                        k = step(dve.tensor_tensor(gated[:, t, :], bank[:, t * C:(t + 1) * C], gate_sb[:, i - 1, :],
                                                   ALU.mult))
                    after(b, k)
                    dve.sem_inc(gated_ready.sem, 1)
                    dve.sem_inc(free, 1)
            assert count[0] == dve_step.per, count


_INS = ['x', 'ctx_1024', 'cond_1024', 'L0_xcond_Wq', 'L0_xcond_bq', 'L0_xcond_Wkv', 'L0_xcond_bkv', 'L0_xcond_Wp',
        'L0_xcond_bp', 'L0_xcond_Wss_q', 'L0_xcond_bss_q', 'L0_xcond_Wss_kv', 'L0_xcond_bss_kv', 'L1_xcond_w_ada',
        'L1_xcond_b_ada', 'L1_xcond_w_qkv', 'L1_xcond_b_qkv', 'L1_xcond_w_so', 'L1_xcond_b_so', 'L1_xcond_w_q',
        'L1_xcond_b_q', 'L1_xcond_w_kv', 'L1_xcond_b_kv', 'L1_xcond_w_co', 'L1_xcond_b_co', 'L1_xcond_w_m1',
        'L1_xcond_b_m1', 'L1_xcond_w_m2', 'L1_xcond_b_m2']
_OUTS = [((16, 256, 256), 'float32')]


def kernel(**inputs):
    import numpy as _np
    import concourse.bacc as _bacc
    from concourse import mybir as _mybir
    from concourse.bass_utils import run_bass_kernel_spmd as _run

    nc = _bacc.Bacc("TRN2", target_bir_lowering=False, num_devices=1)
    arrays, args = {}, []
    for name in _INS:
        a = _np.ascontiguousarray(inputs[name])
        arrays[f"in_{name}_dram"] = a
        args.append(nc.dram_tensor(f"in_{name}_dram", a.shape, _mybir.dt.from_np(a.dtype), kind="ExternalInput").ap())
    for i, (shape, dtype) in enumerate(_OUTS):
        dt = _mybir.dt.from_np(_np.dtype(dtype))
        args.append(nc.dram_tensor(f"out_{i}_dram", shape, dt, kind="ExternalOutput").ap())
    build(nc, *args)
    r = _run(nc, [arrays], core_ids=[0])
    return r.results[0]["out_0_dram"]
```

```python
from contextlib import ExitStack

import concourse.bass as bass
from concourse import mybir

F32 = mybir.dt.float32
BF16 = mybir.dt.bfloat16
FP8 = mybir.dt.float8e4
ALU = mybir.AluOpType
ACT = mybir.ActivationFunctionType
AX_X = mybir.AxisListType.X

P = 128
BIG = 1e30
CROSS, SELF, TOPK = 0, 1, 2
Q_PARTS = (0, 0, 0, 1, 1, 2)
K_PARTS = (0, 1, 2, 0, 1, 0)
LAG = {"A+": 0, "A": 1, "B+": 1, "B": 2, "C+": 2, "C": 3, "D+": 3, "D": 4}
TENSORS = ("k2", "q2", "q0", "k0", "q1", "k1")
STAGE_OF = {"k2": "C", "q2": "C", "q0": "A", "k0": "A", "q1": "B", "k1": "B"}

SCHEDULE = [
    ("stats", "C", 2), ("stats", "D", 3), ("turn", "C", "tr"), ("norm_x", "C", 2), ("turn", "C", "th2"),
    ("base", "C", 2), ("stats", "A", 0), ("stats", "B", 1), ("norm_x", "A", 0), ("project", "C", "k2"),
    ("norm_x", "B", 1), ("split", "C", "k2"), ("project", "C", "q2"), ("value", "C", 2), ("turn", "A", "tx"),
    ("norm_x", "D", 3), ("split", "C", "q2"), ("turn", "A", "tc"), ("project", "A", "q0"), ("unstack", "C", "k2"),
    ("split", "A", "q0"), ("turn", "B", "th1"), ("project", "A", "k0"), ("unstack", "C", "q2"),
    ("split", "A", "k0"), ("unstack", "A", "q0"), ("turn", "D", "th3"), ("project", "B", "q1"), ("hidden", "D", 0),
    ("unstack", "A", "k0"), ("split", "B", "q1"), ("project", "B", "k1"), ("hidden", "D", 1), ("split", "B", "k1"),
    ("hidden", "D", 2), ("value", "A", 0), ("score", "A", (0, 0)), ("score", "A", (0, 1)), ("score", "A", (0, 2)),
    ("score", "A", (0, 3)), ("score", "A", (0, 4)), ("hidden", "D", 3), ("score", "A", (0, 5)),
    ("score", "A", (0, 6)), ("unstack", "B", "q1"), ("hidden", "D", 4), ("score", "A", (0, 7)),
    ("unstack", "B", "k1"), ("value", "B", 1), ("score", "A", (0, 8)), ("max_rows", "A", (0, 0)),
    ("score", "B", (1, 0)), ("score", "B", (1, 1)), ("base", "A", 0), ("score", "B", (1, 2)),
    ("score", "A", (0, 9)), ("score", "B", (1, 3)), ("score", "A", (0, 10)), ("score", "C", (2, 0)),
    ("score", "C", (2, 1)), ("score", "B", (1, 4)), ("hidden", "D", 5), ("base", "D", 3), ("base", "B", 1),
    ("score", "A", (0, 11)), ("hidden", "D", 6), ("score", "A", (0, 12)), ("hidden", "D", 7), ("exp", "A", (0, 0)),
    ("score", "A", (0, 13)), ("score", "A", (0, 14)), ("exp", "A", (0, 1)), ("score", "C", (2, 2)),
    ("score", "A", (0, 15)), ("attend", "A", (0, 0)), ("score", "B", (1, 5)), ("exp", "A", (0, 2)),
    ("max_rows", "A", (0, 1)), ("score", "B", (1, 6)), ("score", "C", (2, 3)), ("exp", "A", (0, 3)),
    ("score", "B", (1, 7)), ("score", "C", (2, 4)), ("attend", "A", (0, 1)), ("attend", "A", (0, 2)),
    ("exp", "A", (0, 4)), ("score", "C", (2, 5)), ("attend", "A", (0, 3)), ("exp", "A", (0, 5)),
    ("attend", "A", (0, 4)), ("max_rows", "B", (1, 0)), ("score", "C", (2, 6)), ("exp", "A", (0, 6)),
    ("score", "C", (2, 7)), ("attend", "A", (0, 5)), ("score", "C", (2, 8)), ("divide", "A", (0, 0)),
    ("out", "D", 3), ("exp", "A", (0, 7)), ("score", "C", (2, 9)), ("attend", "A", (0, 6)), ("attend", "A", (0, 7)),
    ("exp", "B", (1, 0)), ("score", "C", (2, 10)), ("exp", "B", (1, 1)), ("attend", "B", (1, 0)),
    ("max_rows", "C", (2, 0)), ("divide", "A", (0, 1)), ("exp", "B", (1, 2)), ("score", "C", (2, 11)),
    ("attend", "B", (1, 1)), ("exp", "B", (1, 3)), ("score", "C", (2, 12)), ("divide", "B", (1, 0)),
    ("attend", "B", (1, 2)), ("exp", "C", (2, 0)), ("score", "C", (2, 13)), ("attend", "B", (1, 3)),
    ("exp", "C", (2, 1)), ("score", "C", (2, 14)), ("exp", "C", (2, 2)), ("score", "C", (2, 15)),
    ("attend", "C", (2, 0)), ("attend", "C", (2, 1)), ("max_rows", "C", (2, 1)), ("exp", "C", (2, 3)),
    ("attend", "C", (2, 2)), ("divide", "B", (1, 1)), ("out", "B", 1), ("attend", "C", (2, 3)),
    ("exp", "C", (2, 4)), ("exp", "C", (2, 5)), ("fetch", "D+", "D"), ("attend", "C", (2, 4)), ("exp", "C", (2, 6)),
    ("attend", "C", (2, 5)), ("exp", "C", (2, 7)), ("attend", "C", (2, 6)), ("divide", "C", (2, 0)),
    ("attend", "C", (2, 7)), ("divide", "C", (2, 1)), ("out", "A", 0), ("out", "C", 2), ("fetch", "B+", "B"),
    ("fetch", "C+", "C"), ("fetch", "A+", "A"),
]


class Signal:

    def __init__(self, sem, per, seed=0, unit=1):
        self.sem, self.per, self.seed, self.unit = sem, per, seed, unit

    def at(self, b, k=1):
        return self.sem, b * (self.per * self.unit) + (self.seed + k) * self.unit

    def before(self, b, k=1):
        assert self.seed >= self.per
        return self.sem, b * (self.per * self.unit) + (self.seed + k - self.per) * self.unit

    def room(self, b, n):
        return self.sem, b * self.per + n + 1


def build(nc, x, ctx_in, cond, Wq, bq, Wkv, bkv, Wp, bp, Wss_q, bss_q, Wss_kv, bss_kv, w_ada, b_ada,
          w_qkv, b_qkv, w_so, b_so, w_q, b_q, w_kv, b_kv, w_co, b_co, w_m1, b_m1, w_m2, b_m2, out):
    B, L, C = x.shape
    H, D = 16, 16
    NT = L // P
    NC = C // P
    HID = w_m2.shape[0]
    NJ = HID // P
    WIN, SHIFT = 128, 64
    HH = H // NC
    SCALE = float(D) ** -0.5
    NPART = 3
    KP = len(Q_PARTS) * D
    KM = KP + 2
    NS = H
    ROOMS = 4

    MODS = [(0, 0, 1), (0, C, 0), (1, 0, 1), (1, C, 0)] + [
        (2, i * C, one) for i, one in ((1, 1), (0, 0), (4, 1), (3, 0), (7, 1), (6, 0))]
    MOD_OF = {"tx": 0, "tc": 2, "th1": 4, "th2": 6, "th3": 8}
    MOD_USERS = {"A": ("tx", "tc"), "B": ("th1",), "C": ("th2",), "D": ("th3",)}
    MOD_COLS = {"A": (0, 4 * NC), "B": (4 * NC, 6 * NC), "C": (6 * NC, 8 * NC), "D": (8 * NC, 10 * NC)}
    BIAS = [(bss_q, 0, 2 * C), (bss_kv, 0, 2 * C), (b_ada, 0, 9 * C), (bq, 0, C), (bkv, 0, C),
            (b_qkv, 0, 2 * C), (b_q, 0, C), (b_kv, 0, C), (b_m1, 0, 2 * HID)]
    row, BROW = 0, []
    for _, _, n in BIAS:
        BROW.append(row)
        row += n // P
    NROW = row
    R_SSQ, R_SSKV, R_ADA, R_Q0, R_K0, R_QK1, R_Q2, R_K2, R_M1 = BROW

    def exp_units(a):
        units = []
        for hh in range(NC):
            for kb in range(NT):
                for par in range(2):
                    heads = [2 * j + par for j in range(HH // 2)]
                    units += [(hh, kb, heads)] if a == SELF else [(hh, kb, heads[0:2]), (hh, kb, heads[2:4])]
        return units

    UNITS = [exp_units(a) for a in range(3)]

    def live(i):
        return [s for s in LAG if 0 <= i - LAG[s] < B]

    def events(stages):
        ev = {"pj": [], "s": [], "e": [], "od": []}
        for kind, stage, arg in SCHEDULE:
            if stage not in stages:
                continue
            if kind in ("turn", "project"):
                ev["pj"].append(arg)
            if kind == "value":
                ev["pj"].append(f"v{arg}")
            if kind == "hidden":
                ev["pj"].append(f"h{arg}")
            if kind == "out":
                ev["pj"].append(f"o{arg}")
            if kind == "max_rows":
                ev["pj"].append(("m",) + arg)
            if kind == "score":
                ev["s"].append(arg)
            if kind == "exp":
                a, g = arg
                ev["e"] += [(a, 2 * g), (a, 2 * g + 1)]
            if kind == "attend":
                a, g = arg
                hh = UNITS[a][2 * g][0]
                if (a, hh) not in ev["od"]:
                    ev["od"].append((a, hh))
        return ev

    ROUNDS = B + max(LAG.values())
    FIRST = max(LAG.values())
    LOOPED = B - FIRST
    FULL = {k: len(v) for k, v in events(LAG).items()}
    assert FULL["pj"] % 2 == 0 and FULL["s"] % 2 == 0 and FULL["e"] % ROOMS == 0 and FULL["od"] % 2 == 0

    class Round:

        def __init__(self, i, j, start, stages):
            self.i, self.j, self.start, self.stages = i, j, dict(start), stages
            self.names = events(stages)
            self.order = {k: {name: n for n, name in enumerate(v)} for k, v in self.names.items()}

        def batch(self, stage):
            return self.i - LAG[stage]

        def number(self, ring, name):
            return self.start[ring] + self.order[ring][name]

        def count(self, ring, n):
            return n if self.j is None else self.j * FULL[ring] + n

    def rounds(eng, handlers):
        start = {k: 0 for k in FULL}

        def emit(i, j, stages):
            r = Round(i, j, start, stages)
            for kind, stage, arg in SCHEDULE:
                if stage in stages and kind in handlers:
                    handlers[kind](r, r.batch(stage), arg)
            for k, v in r.names.items():
                start[k] += len(v)

        for i in range(FIRST):
            emit(i, None, live(i))
        with eng.Fori(0, LOOPED) as j:
            emit(j + FIRST, j, list(LAG))
        for k in start:
            start[k] += (LOOPED - 1) * FULL[k]
        for i in range(FIRST + LOOPED, ROUNDS):
            emit(i, None, live(i))

    SETUP_POOL = 12
    SETUP_DVE = 8 + len(MODS) * NC + 6

    with ExitStack() as ctx:
        def sb(name, shape, dt=F32):
            return ctx.enter_context(nc.sbuf_tensor(name, shape, dt))

        def sem(name):
            return ctx.enter_context(nc.semaphore(name))

        seeds = []

        def signal(name, per=1, seed=0, unit=1):
            s = Signal(sem(name), per, seed, unit)
            if seed:
                seeds.append(s)
            return s

        parts_dram = {t: nc.dram_tensor(f"parts_{t}", (NPART, C, L), BF16, kind="Internal").ap() for t in TENSORS}
        gates_dram = nc.dram_tensor("gates_scratch", (B, 6 * C), F32, kind="Internal").ap()

        W, loads, setup_loads = {}, [], []
        full = sb("full", [P, 2, NC, L])
        left = sb("left", [P, 2, 2, L])
        hid = sb("hid", [P, NJ, L])
        prob = sb("prob", [P, ROOMS, 512])
        xn = sb("xn", [P, 6, C])
        shared = sb("shared", [P, NC * 9 * C])
        W["wss0"] = full[:].rearrange("p s c l -> p (s c l)").rearrange("p (c n) -> p c n", c=NC)
        W["wss1"] = left[:].rearrange("p s c l -> p (s c l)").rearrange("p (c n) -> p c n", c=NC)
        W["ada"] = shared[:].rearrange("p (c n) -> p c n", c=NC)
        n_other = NT * H * L // 4
        other = shared[:, 0:n_other].bitcast(FP8).rearrange("p (t h n) -> p t h n", t=NT, h=H)
        pieces = [shared[:, n_other + i * NT * C:n_other + (i + 1) * NT * C].rearrange("p (t c) -> p t c", t=NT)
                  for i in range(5)]
        gated, base1, base2, th, ub = pieces
        gate_bias = hid[0:B, 0:6, :]
        gates = prob[0:B].rearrange("b s n -> b (s n)")[:, 0:6 * C].rearrange("b (g c) -> b g c", g=6)
        cond_sb, cond_t, silu_c = xn[0:B, 0, :], xn[0:B, 1, :], xn[0:B, 2, :]
        for name, w in (("wss0", Wss_q), ("wss1", Wss_kv), ("ada", w_ada)):
            setup_loads.append((W[name], w.rearrange("(c p) n -> p c n", p=P)))
        for name, w in (("q0", Wq), ("kv0", Wkv), ("p0", Wp), ("qkv1", w_qkv), ("p1", w_so), ("q2", w_q),
                        ("kv2", w_kv), ("p2", w_co), ("m1", w_m1), ("m2", w_m2)):
            k, n = w.shape
            W[name] = sb("w_" + name, [P, k // P, n])
            loads.append((W[name][:], w.rearrange("(c p) n -> p c n", p=P)))
        bias_rows = hid[0:NROW, 6, 0:P]
        for (v, o, n), r in zip(BIAS, BROW):
            setup_loads.append((bias_rows[r:r + n // P, :], v[o:o + n].rearrange("(r p) -> r p", p=P)))
        vb = sb("vb", [P, 4, C])
        for i, v in enumerate((bkv[C:2 * C], b_qkv[2 * C:3 * C], b_kv[C:2 * C], bp)):
            loads.append((vb[:, i, :], v.partition_broadcast(P)))
        for i, v in enumerate([b_ada[g * C:(g + 1) * C] for g in (2, 5, 8)] + [b_so, b_co, b_m2]):
            setup_loads.append((gate_bias[:, i, :], v.partition_broadcast(B)))
        setup_loads.insert(0, (cond_sb, cond))

        ident = sb("ident", [P, P])
        identb = sb("identb", [P, P], BF16)
        negbig = sb("negbig", [P, P], BF16)
        ones2 = sb("ones2", [P, 2, 2 * D])
        neg_half = sb("neg_half", [P, 4])
        silu_T = xn[:, 3, 0:NC * B].rearrange("p (c b) -> p c b", c=NC)
        bias_col = sb("bias_col", [P, NROW])
        half_col = sb("half_col", [P, 2 * NJ])
        q_col = sb("q_col", [P, 3, NC])
        mod = sb("mod", [P, B, len(MODS) * NC])
        x_sb = sb("x_sb", [P, NT, C])
        c_sb = sb("c_sb", [P, NT, C])
        c2_sb = sb("c2_sb", [P, NT, C])
        gate = {s: sb(f"gate{s}", [P, 2, C]) for s in "BCD"}
        mod_b = sb("mod_b", [P, len(MODS) * NC])
        stats = sb("stats", [P, 4, 4, 6])
        mv = sb("mv", [P, 4, 4, 2])
        var_eps = sb("var_eps", [P, 4, 4])
        rstd = sb("rstd", [P, 4, 4])
        XN = {2: 0, 1: 0, 0: 2, 3: 2}
        hT = sb("hT", [P, 5, NC, L])
        HT = {"tr": 0, "th2": 1, "tx": 2, "tc": 3, "th1": 0, "th3": 4}
        parts = sb("parts", [P, 2, NPART, NC, L], BF16)
        TQ = [sb(f"TQ{a}", [P, H, L], BF16) for a in range(3)]
        TK = [sb(f"TK{a}", [P, H, L], BF16) for a in range(3)]
        V = [sb(f"V{a}", [P, NT, H * 2 * D]) for a in range(3)]
        mx = [sb(f"mx{a}", [P, NT, H]) for a in range(2)]
        top1 = sb("top1", [P, NT, H, 8])
        top2 = sb("top2", [P, 2, 2, 8])
        negm = [sb(f"negm{a}", [P, 2, 2, NT, HH], BF16) for a in range(3)]
        negmT = [sb(f"negmT{a}", [2 * NT * HH, 2, P], BF16) for a in range(3)]
        rsum = sb("rsum", [P, L])
        ON = [sb(f"ON{a}", [P, NC, L]) for a in range(3)]
        res = [sb(f"res{i}", [P, NT, C]) for i in range(3)]
        base = [x_sb[:], base1, base2, res[2][:]]

        pj = [ctx.enter_context(nc.psum_tensor(f"pj{i}", [P, 512], F32)) for i in range(2)]
        ps = [ctx.enter_context(nc.psum_tensor(f"ps{i}", [P, 512], F32)) for i in range(2)]
        pt = [ctx.enter_context(nc.psum_tensor(f"pt{i}", [P, 512], F32)) for i in range(2)]
        po = [ctx.enter_context(nc.psum_tensor(f"po{i}", [P, 512], F32)) for i in range(2)]

        setup_in = sem("setup_in")
        w_in = sem("w_in")
        setup_pool = sem("setup_pool")
        setup_act = sem("setup_act")
        setup_pe = sem("setup_pe")
        setup_dve = sem("setup_dve")
        gates_out = sem("gates_out")
        settled = {}
        pj_full = [signal(f"pj_full{i}") for i in range(2)]
        pj_free = [signal(f"pj_free{i}", 1, 1) for i in range(2)]
        s_full = signal("s_full")
        s_free = signal("s_free", 1, 2)
        st_full = signal("st_full")
        e_done = signal("e_done", 1, 2)
        pv_done = signal("pv_done", 1, ROOMS)
        od_free = signal("od_free", 1, 2)
        x_in = signal("x_in", unit=16)
        c_in = signal("c_in", unit=16)
        c2_in = signal("c2_in", unit=16)
        gate_in = {s: signal(f"gate_in{s}", unit=16) for s in "BCD"}
        mod_in = {s: signal(f"mod_in{s}") for s in "ABCD"}
        bn_done = [signal(f"bn_done{n}") for n in range(4)]
        mv_done = [signal(f"mv_done{n}") for n in range(4)]
        eps_done = [signal(f"eps_done{n}") for n in range(4)]
        rstd_done = [signal(f"rstd_done{n}") for n in range(4)]
        xn_done = [signal(f"xn_done{n}") for n in range(4)]
        part1 = {t: signal(f"part1_{t}") for t in TENSORS}
        rest1 = {t: signal(f"rest1_{t}") for t in TENSORS}
        part2 = {t: signal(f"part2_{t}") for t in TENSORS}
        part3 = {t: signal(f"part3_{t}") for t in TENSORS}
        parts_out = {t: signal(f"parts_out_{t}", unit=16) for t in TENSORS}
        parts_in = {t: signal(f"parts_in_{t}", 6, 6, unit=16) for t in TENSORS}
        negm_hi = [signal(f"negm_hi{a}", 2) for a in range(3)]
        negm_done = [signal(f"negm_done{a}", 2) for a in range(3)]
        m_in = [[signal(f"m_in{a}_{c}", 2 * NT, unit=16) for c in range(2)] for a in range(3)]
        top_step = signal("top_step", 6 * NS)
        left_done = signal("left_done", NS)
        other_done = signal("other_done", NS, 2)
        recip_done = [signal(f"recip_done{a}", 2) for a in range(3)]
        base_done = [signal(f"base_done{i}") for i in range(4)]
        gated_done = [signal(f"gated_done{i}") for i in range(4)]
        res_done = [signal(f"res_done{i}") for i in range(4)]
        tanh_done = signal("tanh_done", NJ)
        hid_done = signal("hid_done", NJ, 2)
        y_out = signal("y_out", 1, 1, 16)

        def need(eng, *waits, settle=False):
            vals = [(s, v if isinstance(v, int) else eng.snap(v)) for s, v in waits]
            own = settled.get(id(eng))
            for n, (s, v) in enumerate(vals):
                eng.wait_ge(s, v)
                if own is not None and (own[1] or settle and n == len(vals) - 1):
                    eng.sem_inc(own[0], 1)

        def can_settle(eng, name, always=False):
            settled[id(eng)] = (sem(name), always)

        def pj_bank(r, name):
            return pj[r.number("pj", name) % 2]

        def pj_at(r, sig, name, k):
            n = r.number("pj", name)
            v = n // 2 + k
            return sig[n % 2].sem, v if r.j is None else r.j * (FULL["pj"] // 2) + v

        def pj_written(r, name):
            return pj_at(r, pj_full, name, 1)

        def pj_read(r, name):
            return pj_at(r, pj_free, name, 2)

        def pj_room(r, name):
            return pj_at(r, pj_free, name, 1)

        def slot_before(r, t):
            n = TENSORS.index(t)
            for back in (2, 4, 6):
                p = TENSORS[(n - back) % 6]
                rounds_ago = 0 if n - back >= 0 else 1
                b = r.batch(STAGE_OF[p]) - rounds_ago
                if r.j is not None or 0 <= b < B:
                    return [parts_out[p].at(b)]
            return []

        LN_SRC = [x_sb, res[0], res[1], res[2]]
        LN_EPS = [1e-5, 1e-6, 1e-6, 1e-6]

        block = ctx.enter_context(nc.Block())

        @block.sync
        def _(sp):
            can_settle(sp, "settled_sp", always=True)
            for dst, src in setup_loads:
                sp.dma_start(dst, src).then_inc(setup_in, 16)
            for dst, src in loads:
                sp.dma_start(dst, src).then_inc(w_in, 16)
            gates_stored = []

            def store_gates():
                sp.wait_ge(setup_dve, SETUP_DVE)
                sp.dma_start(gates_dram, gates.rearrange("b g c -> b (g c)")).then_inc(gates_out, 16)
                sp.wait_ge(gates_out, 16)
                gates_stored.append(True)

            def store_parts(r, b, t):
                need(sp, part3[t].at(b),
                     parts_in[t].before(b, 6))
                sp.dma_start(parts_dram[t].rearrange("i (m p) n -> p i m n", p=P), parts[:, TENSORS.index(t) % 2]
                             ).then_inc(parts_out[t].sem, 16)

            def stack_parts(r, b, t):
                a, isq = int(t[1]), t[0] == "q"
                need(sp, parts_out[t].at(b))
                for i, part in enumerate(Q_PARTS if isq else K_PARTS):
                    sp.dma_start((TQ if isq else TK)[a][i * D:(i + 1) * D, :, :],
                                 parts_dram[t][part].rearrange("(h d) n -> d h n", d=D)).then_inc(parts_in[t].sem, 16)

            def max_rows(r, b, arg):
                a, hh = arg
                need(sp, pj_read(r, ("m", a, hh)))
                chunks = (hh,) if a != SELF else (0, 1)
                for c in chunks:
                    for i in range(2):
                        for qt in range(NT):
                            row = (i * NT + qt) * HH
                            sp.dma_start(TQ[a][KP + i:KP + i + 1, c * HH:(c + 1) * HH, qt * P:(qt + 1) * P],
                                         negmT[a][row:row + HH, c, :]).then_inc(m_in[a][c].sem, 16)

            def fetch(r, b, stage):
                def gates_of(i):
                    if not gates_stored:
                        store_gates()
                    if stage in r.stages:
                        need(sp, pj_read(r, f"o{i}"), base_done[i].at(b - 1))
                    sp.dma_start(gate[stage][:].rearrange("p n c -> p (n c)"),
                                 gates_dram[b, (i - 1) * 2 * C:i * 2 * C].partition_broadcast(P)
                                 ).then_inc(gate_in[stage].sem, 16)
                if stage == "A":
                    if "A" in r.stages:
                        need(sp, pj_read(r, "o0"), xn_done[0].at(b - 1))
                    sp.dma_start(x_sb[:], x[b].rearrange("(t p) c -> p t c", p=P)).then_inc(x_in.sem, 16)
                    sp.dma_start(c_sb[:], ctx_in[b].rearrange("(t p) c -> p t c", p=P)).then_inc(c_in.sem, 16)
                    if not gates_stored:
                        store_gates()
                if stage == "B":
                    gates_of(1)
                if stage == "C":
                    gates_of(2)
                    if "C" in r.stages:
                        need(sp, pj_written(r, "tr"))
                    sp.dma_start(c2_sb[:], ctx_in[b].rearrange("(t p) c -> p t c", p=P)).then_inc(c2_in.sem, 16)
                if stage == "D":
                    gates_of(3)

            def out_(r, b, i):
                if i == 3:
                    need(sp, res_done[3].at(b))
                    sp.dma_start(out[b].rearrange("(t p) c -> p t c", p=P), res[2][:]).then_inc(y_out.sem, 16)

            rounds(sp, {"split": store_parts, "unstack": stack_parts, "max_rows": max_rows, "fetch": fetch,
                        "out": out_})
            sp.wait_ge(y_out.sem, 16 * (B + 1))
            for t in TENSORS:
                sp.wait_ge(parts_out[t].sem, 16 * B)

        @block.gpsimd
        def _(pool):
            can_settle(pool, "settled_pool")
            pool.memset(ident[:], 0.0).then_inc(setup_pool, 1)
            pool.wait_ge(setup_pool, 1)
            pool.affine_select(out=ident[:], in_=ident[:], compare_op=ALU.not_equal, fill=1.0, base=0,
                               pattern=[[-1, P]], channel_multiplier=1).then_inc(setup_pool, 1)
            pool.memset(neg_half[:], -0.5).then_inc(setup_pool, 1)
            pool.memset(ones2[:], 0.0).then_inc(setup_pool, 1)
            pool.wait_ge(setup_pool, 4)
            pool.memset(ones2[:, 0, 0:D], 1.0).then_inc(setup_pool, 1)
            pool.memset(ones2[:, 1, D:2 * D], 1.0).then_inc(setup_pool, 1)
            for a in range(3):
                pool.memset(V[a][:], 0.0).then_inc(setup_pool, 1)
            for a in range(3):
                pool.wait_ge(setup_pool, SETUP_POOL - 3 + a)
                pool.memset(TK[a][KP:KM, :, :], 1.0).then_inc(setup_pool, 1)
            pool.wait_ge(setup_pool, SETUP_POOL)
            for s in seeds:
                pool.sem_inc(s.sem, s.seed * s.unit)
            pool.wait_ge(w_in, 16 * len(loads))
            pool.wait_ge(setup_dve, SETUP_DVE)

            def rstd_of(r, b, n):
                tiles = 4 if n == 0 else 2
                need(pool, mv_done[n].at(b), settle=True)
                pool.tensor_scalar(var_eps[:, n, 0:tiles], mv[:, n, 0:tiles, 1], LN_EPS[n], None, ALU.add
                                   ).then_inc(eps_done[n].sem, 1)
                need(pool, eps_done[n].at(b))
                pool.tensor_tensor(rstd[:, n, 0:tiles], var_eps[:, n, 0:tiles], neg_half[:, 0:tiles], ALU.pow
                                   ).then_inc(rstd_done[n].sem, 1)

            def first_rest(r, b, t):
                s = TENSORS.index(t) % 2
                need(pool, part1[t].at(b))
                pool.tensor_tensor(full[:, s], full[:, s], parts[:, s, 0], ALU.subtract).then_inc(rest1[t].sem, 1)

            def third_part(r, b, t):
                s = TENSORS.index(t) % 2
                need(pool, part2[t].at(b))
                pool.tensor_tensor(parts[:, s, 2], full[:, s], parts[:, s, 1], ALU.subtract).then_inc(part3[t].sem, 1)

            def base_of(r, b, i):
                if i == 0:
                    need(pool, xn_done[0].at(b))
                else:
                    stage = "ABCD"[i]
                    waits = [gate_in[stage].at(b), res_done[i - 1].at(b)]
                    if i == 3:
                        waits.append(xn_done[3].at(b))
                    need(pool, *waits)
                for t in range(NT):
                    bias = vb[:, 3, :] if i == 0 else gate["ABCD"[i]][:, 1, :]
                    ins = pool.tensor_tensor(base[i][:, t, :], LN_SRC[i][:, t, :], bias, ALU.add)
                ins.then_inc(base_done[i].sem, 1)

            def fetch(r, b, stage):
                if stage in r.stages:
                    need(pool, *[pj_read(r, name) for name in MOD_USERS[stage]])
                lo, hi = MOD_COLS[stage]
                pool.tensor_copy(mod_b[:, lo:hi], mod[:, bass.ds(b, 1), lo:hi].rearrange("p o m -> p (o m)")
                                 ).then_inc(mod_in[stage].sem, 1)

            rounds(pool, {"stats": rstd_of, "project": first_rest, "split": third_part, "base": base_of,
                          "fetch": fetch})

        @block.tensor
        def _(pe):
            can_settle(pe, "settled_pe")
            pe.wait_ge(setup_in, 16 * len(setup_loads))
            pe.wait_ge(setup_pool, SETUP_POOL)
            pe.wait_ge(setup_dve, 2)
            pe.transpose(ps[0][:, 0:NROW], bias_rows, ident[0:NROW, 0:NROW])
            for c in range(NC):
                ins = pe.transpose(ps[1][:, c * B:(c + 1) * B], silu_c[:, c * P:(c + 1) * P], ident[0:B, 0:B])
            ins.then_inc(setup_pe, 1)
            pe.wait_ge(setup_act, 3)
            wmod = [W["wss0"], W["wss1"], W["ada"]]
            for m, (w, o, _) in enumerate(MODS):
                for c in range(NC):
                    for k in range(NC):
                        pe.matmul(po[0][:, (m * NC + c) * B:(m * NC + c + 1) * B],
                                  wmod[w][:, k, o + c * P:o + (c + 1) * P], silu_T[:, k, :],
                                  start=(k == 0), stop=(k == NC - 1))
            for i, g in enumerate((2, 5, 8)):
                dst = pt[i // 2][0:B, (i % 2) * C:(i % 2 + 1) * C]
                for k in range(NC):
                    ins = pe.matmul(dst, silu_T[:, k, :], W["ada"][:, k, g * C:(g + 1) * C],
                                    start=(k == 0), stop=(k == NC - 1))
            ins.then_inc(setup_pe, 1)
            pe.wait_ge(w_in, 16 * len(loads))
            pe.wait_ge(setup_dve, SETUP_DVE)

            def begin(r, name, *waits, settle=False):
                need(pe, pj_room(r, name), *waits, settle=settle)
                return pj_bank(r, name)

            def end(r, name, ins):
                ins.then_inc(pj_full[r.number("pj", name) % 2].sem, 1)

            def turn(r, b, name):
                src, o, wait = {"tr": (c2_sb, 0, c2_in.at(b)), "th2": (xn, 0, xn_done[2].at(b)),
                                "tx": (xn, 2, xn_done[0].at(b)), "tc": (xn, 4, xn_done[0].at(b)),
                                "th1": (xn, 0, xn_done[1].at(b)), "th3": (xn, 2, xn_done[3].at(b))}[name]
                bank = begin(r, name, wait)
                for c in range(NC):
                    for t in range(NT):
                        ins = pe.transpose(bank[:, c * L + t * P:c * L + (t + 1) * P],
                                           src[:, o + t, c * P:(c + 1) * P], ident[:])
                end(r, name, ins)

            def project(r, b, t):
                w, col, src = {"q0": ("q0", 0, "tx"), "k0": ("kv0", 0, "tc"), "q1": ("qkv1", 0, "th1"),
                               "k1": ("qkv1", C, "th1"), "q2": ("q2", 0, "th2"), "k2": ("kv2", 0, "tr")}[t]
                bank = begin(r, t, pj_read(r, src))
                for m in range(NC):
                    for k in range(NC):
                        ins = pe.matmul(bank[:, m * L:(m + 1) * L], W[w][:, k, col + m * P:col + (m + 1) * P],
                                        hT[:, HT[src], k, :], start=(k == 0), stop=(k == NC - 1))
                end(r, t, ins)

            def token_major(r, name, w, col, src, nk, *waits):
                bank = begin(r, name, *waits)
                for t in range(NT):
                    for k in range(nk):
                        ins = pe.matmul(bank[:, t * C:(t + 1) * C], src[:, k, t * P:(t + 1) * P],
                                        W[w][:, k, col:col + C], start=(k == 0), stop=(k == nk - 1))
                end(r, name, ins)

            def value(r, b, a):
                w, col, src = (("kv0", C, "tc"), ("qkv1", 2 * C, "th1"), ("kv2", C, "tr"))[a]
                token_major(r, f"v{a}", w, col, hT[:, HT[src]], NC, pj_read(r, src))

            def score(r, b, arg):
                a, u = arg
                g = r.number("s", arg)
                waits = [s_free.room(0, r.count("s", g))]
                if u == 0:
                    waits += [parts_in[f"q{a}"].at(b, 6), parts_in[f"k{a}"].at(b, 6)]
                need(pe, *waits)
                n = L if a != SELF else WIN
                per = 512 // n
                hp, qt = u // NT, u % NT
                for i in range(per):
                    h = hp * per + i
                    k0 = 0 if a != SELF else qt * WIN
                    ins = pe.matmul(ps[g % 2][:, i * n:(i + 1) * n], TQ[a][0:KP, h, qt * P:(qt + 1) * P],
                                    TK[a][0:KP, h, k0:k0 + n], start=True, stop=True)
                ins.then_inc(s_full.sem, 1)

            def max_rows(r, b, arg):
                a, hh = arg
                name = ("m", a, hh)
                bank = begin(r, name, negm_done[a].at(b, hh + 1 if a != SELF else 2), settle=True)
                rows = 2 * NT * HH
                for c in ((hh,) if a != SELF else (0, 1)):
                    ins = pe.transpose(bank[0:rows, c * P // 2:(c + 1) * P // 2].bitcast(BF16),
                                       negm[a][:, c].rearrange("p i t h -> p (i t h)"), identb[:])
                end(r, name, ins)

            def exp(r, b, arg):
                a, g = arg
                nq = L if a != SELF else WIN
                for n in (2 * g, 2 * g + 1):
                    hh, kb, heads = UNITS[a][n]
                    u = r.number("e", (a, n))
                    waits = [e_done.room(0, r.count("e", u))]
                    half = len(UNITS[a]) // 2
                    if n in (0, half):
                        chunk = 0 if n == 0 else 1
                        waits.append(m_in[a][chunk].at(b, 2 * NT))
                        if a == TOPK:
                            waits.append(other_done.at(b, NS // 2 * (chunk + 1)))
                    need(pe, *waits)
                    for i, h8 in enumerate(heads):
                        h = hh * HH + h8
                        q0 = 0 if a != SELF else kb * WIN
                        ins = pe.matmul(pt[u % 2][:, i * nq:(i + 1) * nq], TK[a][0:KM, h, kb * P:(kb + 1) * P],
                                        TQ[a][0:KM, h, q0:q0 + nq], start=True, stop=True)
                        if a == TOPK:
                            for qt in range(NT):
                                ins = pe.matmul(pt[u % 2][:, i * nq + qt * P:i * nq + (qt + 1) * P],
                                                other[:, qt, h, kb * P:(kb + 1) * P], negbig[:],
                                                start=False, stop=True, skip_group_check=True)
                    ins.then_inc(st_full.sem, 1)

            def attend(r, b, arg):
                a, g = arg
                ns = (2 * g, 2 * g + 1)
                hh = UNITS[a][ns[0]][0]
                nq = L if a != SELF else WIN
                od = r.number("od", (a, hh))
                waits = [e_done.at(0, r.count("e", r.number("e", (a, ns[1])) + 1))]
                first = g % (len(UNITS[a]) // 4) == 0
                if first:
                    waits.append(od_free.room(0, r.count("od", od)))
                if g == 0:
                    waits.append(pj_read(r, f"v{a}"))
                need(pe, *waits)
                seen = set()
                for what in range(2):
                    for n in ns:
                        _, kb, heads = UNITS[a][n]
                        q0 = 0 if a != SELF else kb * WIN
                        for i, h8 in enumerate(heads):
                            h, j = hh * HH + h8, h8 // 2
                            w = ones2[:, h8 % 2, :] if what else V[a][:, kb, h * 2 * D:(h + 1) * 2 * D]
                            ins = pe.matmul(po[od % 2][32 * j:32 * j + 32, what * L + q0:what * L + q0 + nq], w,
                                            prob[:, r.number("e", (a, n)) % ROOMS, i * nq:(i + 1) * nq],
                                            start=first and j not in seen, stop=True, skip_group_check=True)
                            seen.add(j)
                        if what:
                            ins.then_inc(pv_done.sem, 1)

            def out_(r, b, i):
                if i == 3:
                    token_major(r, "o3", "m2", 0, hid, NJ, hid_done.at(b, NJ))
                else:
                    token_major(r, f"o{i}", f"p{i}", 0, ON[i], NC,
                                od_free.at(0, r.count("od", r.number("od", (i, 1)) + 1)))

            def hidden(r, b, j):
                name = f"h{j}"
                bank = begin(r, name, *([pj_read(r, "th3")] if j == 0 else []))
                for half in range(2):
                    for k in range(NC):
                        ins = pe.matmul(bank[:, half * L:(half + 1) * L],
                                        W["m1"][:, k, half * HID + j * P:half * HID + (j + 1) * P],
                                        hT[:, HT["th3"], k, :], start=(k == 0), stop=(k == NC - 1))
                end(r, name, ins)

            rounds(pe, {"turn": turn, "project": project, "value": value, "score": score, "max_rows": max_rows,
                        "exp": exp, "attend": attend, "out": out_, "hidden": hidden})

        @block.scalar
        def _(act):
            can_settle(act, "settled_act")
            act.wait_ge(setup_in, 16 * len(setup_loads))
            act.activation(cond_t, cond_sb, ACT.Tanh, scale=0.5).then_inc(setup_act, 1)
            act.wait_ge(setup_pe, 1)
            act.activation(bias_col[:], ps[0][:, 0:NROW], ACT.Copy).then_inc(setup_act, 1)
            act.activation(silu_T[:].rearrange("p c b -> p (c b)"), ps[1][:, 0:NC * B], ACT.Copy).then_inc(setup_act, 1)
            act.wait_ge(gates_out, 16)

            def freed(r, name):
                return pj_free[r.number("pj", name) % 2].sem

            def turn(r, b, name):
                stage = {"tr": "C", "th2": "C", "tx": "A", "tc": "A", "th1": "B", "th3": "D"}[name]
                waits = [pj_written(r, name)]
                if name != "tr":
                    waits.append(mod_in[stage].at(b))
                if name == "th1" and "C" in r.stages:
                    waits.append(pj_written(r, "v2"))
                need(act, *waits)
                bank = pj_bank(r, name)
                m = MOD_OF.get(name)
                for c in range(NC):
                    kw = {} if m is None else dict(scale=mod_b[:, m * NC + c:m * NC + c + 1],
                                                   bias=mod_b[:, (m + 1) * NC + c:(m + 1) * NC + c + 1])
                    pieces = ((0, L, 0),) if name != "th1" else ((SHIFT, L, 0), (0, SHIFT, L - SHIFT))
                    for lo, hi, to in pieces:
                        ins = act.activation(hT[:, HT[name], c, to:to + hi - lo], bank[:, c * L + lo:c * L + hi],
                                             ACT.Identity if m is not None else ACT.Copy, **kw)
                ins.then_inc(freed(r, name), 1)

            def project(r, b, t):
                a = int(t[1])
                need(act, pj_written(r, t), *slot_before(r, t))
                bank = pj_bank(r, t)
                for m in range(NC):
                    if t[0] == "q":
                        kw = dict(scale=SCALE, bias=q_col[:, a, m:m + 1])
                    else:
                        row = (R_K0, R_QK1 + NC, R_K2)[a] + m
                        kw = dict(bias=bias_col[:, row:row + 1])
                    ins = act.activation(full[:, TENSORS.index(t) % 2, m, :], bank[:, m * L:(m + 1) * L],
                                         ACT.Identity, **kw)
                ins.then_inc(freed(r, t), 1)

            def max_rows(r, b, arg):
                a, hh = arg
                name = ("m", a, hh)
                need(act, pj_written(r, name))
                rows = 2 * NT * HH
                for c in ((hh,) if a != SELF else (0, 1)):
                    ins = act.activation(negmT[a][:, c, :], pj_bank(r, name)[0:rows, c * P // 2:(c + 1) * P // 2]
                                         .bitcast(BF16), ACT.Copy)
                ins.then_inc(freed(r, name), 1)

            def exp(r, b, arg):
                a, g = arg
                for n in (2 * g, 2 * g + 1):
                    u = r.number("e", (a, n))
                    need(act, st_full.at(0, r.count("e", u + 1)),
                         pv_done.room(0, r.count("e", u)))
                    act.activation(prob[:, u % ROOMS, :], pt[u % 2][:], ACT.Exp).then_inc(e_done.sem, 1)

            def score(r, b, arg):
                a, u = arg
                if a == TOPK:
                    need(act, left_done.at(b, u + 1), settle=True)
                    hp, qt = u // NT, u % NT
                    act.activation(other[:, qt, 2 * hp:2 * hp + 2, :], left[:, u % 2], ACT.Relu,
                                   bias=1.0, scale=1.0 / BIG, saturate=False).then_inc(other_done.sem, 1)

            def hidden(r, b, j):
                s = j % 2
                need(act, pj_written(r, f"h{j}"), hid_done.room(b, j))
                bank = pj_bank(r, f"h{j}")
                act.activation(th[:, s, :], bank[:, 0:L], ACT.Tanh, scale=0.5, bias=half_col[:, j:j + 1])
                act.activation(ub[:, s, :], bank[:, L:2 * L], ACT.Identity, scale=0.5,
                               bias=half_col[:, NJ + j:NJ + j + 1]).then_inc(tanh_done.sem, 1)

            rounds(act, {"turn": turn, "project": project, "max_rows": max_rows, "exp": exp, "score": score,
                         "hidden": hidden})

        @block.vector
        def _(dve):
            can_settle(dve, "settled_dve")
            done = [0]

            def setup(ins, read_next=False):
                done[0] += 1
                ins.then_inc(setup_dve, 1)
                if read_next:
                    dve.wait_ge(setup_dve, done[0])

            dve.wait_ge(setup_act, 1)
            setup(dve.scalar_tensor_tensor(out=silu_c, in0=cond_t, scalar=1.0, in1=cond_sb,
                                           op0=ALU.add, op1=ALU.mult), read_next=True)
            setup(dve.tensor_scalar(silu_c, silu_c, 0.5, None, ALU.mult))
            dve.wait_ge(setup_pool, SETUP_POOL)
            setup(dve.tensor_copy(identb[:], ident[:]))
            setup(dve.tensor_scalar(negbig[:], ident[:], -BIG, None, ALU.mult))
            dve.wait_ge(setup_act, 3)
            dve.wait_ge(setup_pe, 2)
            for a, r in enumerate((R_Q0, R_QK1, R_Q2)):
                setup(dve.tensor_scalar(q_col[:, a, :], bias_col[:, r:r + NC], SCALE, None, ALU.mult))
            setup(dve.tensor_scalar(half_col[:], bias_col[:, R_M1:R_M1 + 2 * NJ], 0.5, None, ALU.mult))
            for m, (w, o, one) in enumerate(MODS):
                for c in range(NC):
                    r = (R_SSQ, R_SSKV, R_ADA)[w] + o // P + c
                    i = m * NC + c
                    setup(dve.tensor_scalar(mod[:, :, i], po[0][:, i * B:(i + 1) * B], bias_col[:, r:r + 1],
                                            float(one), ALU.add, ALU.add))
            for i in range(3):
                setup(dve.tensor_tensor(gates[:, 2 * i, :], pt[i // 2][0:B, (i % 2) * C:(i % 2 + 1) * C],
                                        gate_bias[:, i, :], ALU.add), read_next=True)
                setup(dve.tensor_tensor(gates[:, 2 * i + 1, :], gates[:, 2 * i, :], gate_bias[:, 3 + i, :], ALU.mult))
            assert done[0] == SETUP_DVE
            dve.wait_ge(setup_dve, SETUP_DVE)

            def freed(r, name):
                return pj_free[r.number("pj", name) % 2].sem

            def ln_tiles(n):
                return [LN_SRC[n][:, t, :] for t in range(NT)] + ([c_sb[:, t, :] for t in range(NT)] if n == 0 else [])

            def stats_(r, b, n):
                need(dve, *([x_in.at(b), c_in.at(b)] if n == 0 else [res_done[n - 1].at(b)]))
                for i, t in enumerate(ln_tiles(n)):
                    ins = dve.bn_stats(stats[:, n, i, :], t)
                ins.then_inc(bn_done[n].sem, 1)
                need(dve, bn_done[n].at(b), settle=True)
                for i, t in enumerate(ln_tiles(n)):
                    ins = dve.bn_aggr(mv[:, n, i, :], stats[:, n, i, :])
                ins.then_inc(mv_done[n].sem, 1)

            def norm_x(r, b, n):
                waits = [rstd_done[n].at(b)]
                if n == 1 and "C" in r.stages:
                    waits.append(pj_written(r, "th2"))
                if n == 3 and "A" in r.stages:
                    waits.append(pj_written(r, "tx"))
                need(dve, *waits)
                for i, t in enumerate(ln_tiles(n)):
                    ins = dve.tensor_scalar(xn[:, XN[n] + i, :], t, mv[:, n, i, 0:1], rstd[:, n, i:i + 1],
                                            ALU.subtract, ALU.mult)
                ins.then_inc(xn_done[n].sem, 1)

            def project(r, b, t):
                s = TENSORS.index(t) % 2
                need(dve, pj_read(r, t))
                dve.tensor_copy(parts[:, s, 0], full[:, s]).then_inc(part1[t].sem, 1)

            def split(r, b, t):
                s = TENSORS.index(t) % 2
                need(dve, rest1[t].at(b))
                dve.tensor_copy(parts[:, s, 1], full[:, s]).then_inc(part2[t].sem, 1)

            def value(r, b, a):
                name = f"v{a}"
                need(dve, pj_written(r, name))
                bank = pj_bank(r, name)
                for t in range(NT):
                    dst = V[a][:, t, :].rearrange("p (j i d) -> p j i d", i=4, d=D)[:, :, 0:4:3, :]
                    src = bank[:, t * C:(t + 1) * C].rearrange("p (j i d) -> p j i d", i=2, d=D)
                    bias = vb[:, a, :].rearrange("p (j i d) -> p j i d", i=2, d=D)
                    ins = dve.tensor_tensor(dst, src, bias, ALU.add)
                ins.then_inc(freed(r, name), 1)

            def score(r, b, arg):
                a, u = arg
                g = r.number("s", arg)
                hp, qt = u // NT, u % NT
                full_ = s_full.at(0, r.count("s", g + 1))
                freed_ = s_free.at(0, r.count("s", g + 1))
                if a != TOPK:
                    n = L if a == CROSS else WIN
                    per = 512 // n
                    need(dve, full_)
                    dve.tensor_reduce(mx[a][:, qt, hp * per:(hp + 1) * per],
                                      ps[g % 2][:].rearrange("p (h n) -> p h n", n=n), AX_X, ALU.max
                                      ).then_inc(s_free.sem, 1)
                    return
                k = 6 * u
                need(dve, full_, other_done.room(b, u), settle=True)
                src = [ps[g % 2][:, i * L:(i + 1) * L] for i in range(2)]
                lft = [left[:, u % 2, i, :] for i in range(2)]
                t1 = [top1[:, qt, 2 * hp + i, :] for i in range(2)]
                t2 = [top2[:, u % 2, i, :] for i in range(2)]
                dve.max(t1[0], src[0]).then_inc(top_step.sem, 1)
                dve.max(t1[1], src[1]).then_inc(top_step.sem, 1)
                need(dve, top_step.at(b, k + 1), settle=True)
                dve.match_replace(lft[0], t1[0], src[0], -2 * BIG).then_inc(top_step.sem, 1)
                need(dve, top_step.at(b, k + 2), settle=True)
                dve.match_replace(lft[1], t1[1], src[1], -2 * BIG).then_inc(s_free.sem, 1)
                need(dve, top_step.at(b, k + 3), settle=True)
                dve.max(t2[0], lft[0]).then_inc(top_step.sem, 1)
                need(dve, freed_, settle=True)
                dve.max(t2[1], lft[1]).then_inc(top_step.sem, 1)
                need(dve, top_step.at(b, k + 4), settle=True)
                dve.match_replace(lft[0], t2[0], lft[0], -2 * BIG).then_inc(top_step.sem, 1)
                need(dve, top_step.at(b, k + 5), settle=True)
                dve.match_replace(lft[1], t2[1], lft[1], -2 * BIG).then_inc(left_done.sem, 1)

            def max_rows(r, b, arg):
                a, hh = arg
                last = {CROSS: (CROSS, 8 * hh + 7), SELF: (SELF, 7), TOPK: (TOPK, 8 * hh + 7)}[a]
                need(dve, s_free.at(0, r.count("s", r.number("s", last) + 1)))
                for c in ((hh,) if a != SELF else (0, 1)):
                    m = (top1[:, :, c * HH:(c + 1) * HH, 0] if a == TOPK else mx[a][:, :, c * HH:(c + 1) * HH])
                    dve.tensor_scalar(negm[a][:, c, 0], m, -1.0, None, ALU.mult).then_inc(negm_hi[a].sem, 1)
                    need(dve, negm_hi[a].at(b, c + 1))
                    dve.scalar_tensor_tensor(out=negm[a][:, c, 1], in0=m, scalar=-1.0, in1=negm[a][:, c, 0],
                                             op0=ALU.mult, op1=ALU.subtract).then_inc(negm_done[a].sem, 1)

            def divide(r, b, arg):
                a, hh = arg
                od = r.number("od", arg)
                last = (a, len(UNITS[a]) // 2 * (hh + 1) - 1)
                need(dve, pv_done.at(0, r.count("e", r.number("e", last) + 1)),
                     od_free.at(0, r.count("od", od)))
                dve.reciprocal(rsum[:], po[od % 2][:, L:2 * L]).then_inc(recip_done[a].sem, 1)
                need(dve, recip_done[a].at(b, hh + 1))
                for lo, hi, to in (((0, L, 0),) if a != SELF else ((0, L - SHIFT, SHIFT), (L - SHIFT, L, 0))):
                    ins = dve.tensor_tensor(ON[a][:, hh, to:to + hi - lo], po[od % 2][:, lo:hi], rsum[:, lo:hi],
                                            ALU.mult)
                ins.then_inc(od_free.sem, 1)

            def flat(t):
                return t.rearrange("p t c -> p (t c)")

            def out_(r, b, i):
                name = f"o{i}"
                bank = pj_bank(r, name)
                if i == 0:
                    waits = [pj_written(r, name), base_done[0].at(b)]
                    if "B" in r.stages:
                        waits.append(base_done[1].at(b - 1))
                    need(dve, *waits)
                    dve.tensor_tensor(flat(res[0][:]), bank[:], flat(x_sb[:]), ALU.add).then_inc(freed(r, name), 1)
                    need(dve, pj_read(r, name))
                    dve.sem_inc(res_done[0].sem, 1)
                    return
                need(dve, pj_written(r, name), gate_in["ABCD"[i]].at(b))
                for t in range(NT):
                    ins = dve.tensor_tensor(gated[:, t, :], bank[:, t * C:(t + 1) * C], gate["ABCD"[i]][:, 0, :],
                                            ALU.mult)
                ins.then_inc(freed(r, name), 1)
                waits = [pj_read(r, name), base_done[i].at(b)]
                if i == 1 and "C" in r.stages:
                    waits.append(base_done[2].at(b - 1))
                if i == 2:
                    waits.append(y_out.before(b))
                need(dve, *waits)
                dst = flat(res[i][:] if i < 3 else base[3])
                dve.tensor_tensor(dst, flat(gated), flat(base[i]), ALU.add).then_inc(res_done[i].sem, 1)

            def hidden(r, b, j):
                s = j % 2
                bank = pj_bank(r, f"h{j}")
                need(dve, tanh_done.at(b, j + 1))
                dve.scalar_tensor_tensor(out=ub[:, s, :], in0=bank[:, 0:L], scalar=bias_col[:, R_M1 + j:R_M1 + j + 1],
                                         in1=ub[:, s, :], op0=ALU.add, op1=ALU.mult).then_inc(freed(r, f"h{j}"), 1)
                need(dve, pj_read(r, f"h{j}"))
                dve.scalar_tensor_tensor(out=hid[:, j, :], in0=th[:, s, :], scalar=1.0, in1=ub[:, s, :],
                                         op0=ALU.add, op1=ALU.mult).then_inc(hid_done.sem, 1)

            rounds(dve, {"stats": stats_, "norm_x": norm_x, "project": project, "split": split, "value": value,
                         "score": score, "max_rows": max_rows, "divide": divide, "out": out_, "hidden": hidden})


_INS = ['x', 'ctx_1024', 'cond_1024', 'L0_xcond_Wq', 'L0_xcond_bq', 'L0_xcond_Wkv', 'L0_xcond_bkv', 'L0_xcond_Wp',
        'L0_xcond_bp', 'L0_xcond_Wss_q', 'L0_xcond_bss_q', 'L0_xcond_Wss_kv', 'L0_xcond_bss_kv', 'L1_xcond_w_ada',
        'L1_xcond_b_ada', 'L1_xcond_w_qkv', 'L1_xcond_b_qkv', 'L1_xcond_w_so', 'L1_xcond_b_so', 'L1_xcond_w_q',
        'L1_xcond_b_q', 'L1_xcond_w_kv', 'L1_xcond_b_kv', 'L1_xcond_w_co', 'L1_xcond_b_co', 'L1_xcond_w_m1',
        'L1_xcond_b_m1', 'L1_xcond_w_m2', 'L1_xcond_b_m2']
_OUTS = [((16, 256, 256), 'float32')]


def kernel(**inputs):
    import numpy as _np
    import concourse.bacc as _bacc
    from concourse import mybir as _mybir
    from concourse.bass_utils import run_bass_kernel_spmd as _run

    nc = _bacc.Bacc("TRN2", target_bir_lowering=False, num_devices=1)
    arrays, args = {}, []
    for name in _INS:
        a = _np.ascontiguousarray(inputs[name])
        arrays[f"in_{name}_dram"] = a
        args.append(nc.dram_tensor(f"in_{name}_dram", a.shape, _mybir.dt.from_np(a.dtype), kind="ExternalInput").ap())
    for i, (shape, dtype) in enumerate(_OUTS):
        dt = _mybir.dt.from_np(_np.dtype(dtype))
        args.append(nc.dram_tensor(f"out_{i}_dram", shape, dt, kind="ExternalOutput").ap())
    build(nc, *args)
    r = _run(nc, [arrays], core_ids=[0])
    return r.results[0]["out_0_dram"]
```
